# Optimizing a Trainium2 kernel written in Bass

```python
import numpy as np
import jax
import jax.numpy as jnp

def _softmax(x, axis=-1):
    return jax.nn.softmax(x, axis=axis)

def _gelu(x):
    return jax.nn.gelu(x, approximate=True)

def _silu(x):
    return jax.nn.silu(x)

def _sigmoid(x):
    return jax.nn.sigmoid(x)

def _layernorm(x, axis=-1, eps=1e-05):
    m = jnp.mean(x, axis=axis, keepdims=True)
    v = jnp.var(x, axis=axis, keepdims=True)
    return (x - m) / jnp.sqrt(v + eps)

def _scatter_add(tgt, idx, src, axis=0):
    return tgt.at[idx].add(src)

def _segment_sum(src, seg, n):
    return jax.ops.segment_sum(src, seg, n)
kernel_name = 'mk_seq_postln_d1_jaxref_r4_8a79c0'

def setup_inputs(seed: int=0):
    np.random.seed(seed)
    _w = jnp.asarray

    def _L0_attn_setup():
        import jax, jax.numpy as jnp
        import numpy as np
        from functools import partial
        B_, L_, H_, DIN_, K_, N_, R_ = (2, 512, 256, 512, 4, 16, 64)

        def _selective_scan(x, delta, A, Bm, Cm, D):
            dA = jnp.exp(jnp.einsum('bld,dn->bldn', delta, A))
            dBx = jnp.einsum('bld,bln->bldn', delta * x, Bm)
            b, l, d, n = dA.shape

            def step(z, inp):
                dA_t, dBx_t, c_t = inp
                z = dA_t * z + dBx_t
                y = jnp.einsum('bdn,bn->bd', z, c_t)
                return (z, y)
            z0 = jnp.zeros((b, d, n), x.dtype)
            _, ys = jax.lax.scan(step, z0, (jnp.moveaxis(dA, 1, 0), jnp.moveaxis(dBx, 1, 0), jnp.moveaxis(Cm, 1, 0)))
            y = jnp.moveaxis(ys, 0, 1)
            return y + x * D
        key = jax.random.key(seed)
        ks = jax.random.split(key, 9)
        s = lambda f: 1.0 / f ** 0.5
        A = jnp.tile(jnp.arange(1, N_ + 1, dtype=jnp.float32)[None, :], (DIN_, 1))
        return {'hidden_states': jax.random.normal(ks[0], (B_, L_, H_), jnp.float32), 'w_in': jax.random.normal(ks[1], (2 * DIN_, H_), jnp.float32) * s(H_), 'w_conv': jax.random.normal(ks[2], (DIN_, 1, K_), jnp.float32) * s(DIN_), 'w_xproj': jax.random.normal(ks[3], (R_ + 2 * N_, DIN_), jnp.float32) * s(DIN_), 'w_dt': jax.random.normal(ks[4], (DIN_, R_), jnp.float32) * s(R_), 'b_dt': jnp.zeros((DIN_,), jnp.float32), 'A_log': jnp.log(A), 'D': jnp.ones((DIN_,), jnp.float32), 'w_out': jax.random.normal(ks[5], (H_, DIN_), jnp.float32) * s(DIN_)}
    _L0_attn_in = _L0_attn_setup()

    def _L0_ffn_setup():
        import jax, jax.numpy as jnp
        import numpy as np
        NUM_HEADS = 16
        TOP_K = 2
        key = jax.random.key(seed)
        ks = jax.random.split(key, 5)
        B, S, D, E = (4, 512, 256, 8)
        scale = 0.02
        return {'x': jax.random.normal(ks[0], (B, S, D), dtype=jnp.float32), 'W_qkv': jax.random.normal(ks[1], (D, 3 * D), dtype=jnp.float32) * scale, 'b_qkv': jnp.zeros((3 * D,), dtype=jnp.float32), 'W_gate': jax.random.normal(ks[2], (D, E), dtype=jnp.float32) * scale, 'b_gate': jnp.zeros((E,), dtype=jnp.float32), 'W_experts': jax.random.normal(ks[3], (E, D, D), dtype=jnp.float32) * scale, 'b_experts': jnp.zeros((E, D), dtype=jnp.float32)}
    _L0_ffn_in = _L0_ffn_setup()
    _d = {'L0_attn_hidden_states': _L0_attn_in['hidden_states'], 'L0_attn_w_in': _L0_attn_in['w_in'], 'L0_attn_w_conv': _L0_attn_in['w_conv'], 'L0_attn_w_xproj': _L0_attn_in['w_xproj'], 'L0_attn_w_dt': _L0_attn_in['w_dt'], 'L0_attn_b_dt': _L0_attn_in['b_dt'], 'L0_attn_A_log': _L0_attn_in['A_log'], 'L0_attn_D': _L0_attn_in['D'], 'L0_attn_w_out': _L0_attn_in['w_out'], 'L0_ffn_W_qkv': _L0_ffn_in['W_qkv'], 'L0_ffn_b_qkv': _L0_ffn_in['b_qkv'], 'L0_ffn_W_gate': _L0_ffn_in['W_gate'], 'L0_ffn_b_gate': _L0_ffn_in['b_gate'], 'L0_ffn_W_experts': _L0_ffn_in['W_experts'], 'L0_ffn_b_experts': _L0_ffn_in['b_experts']}
    _x0 = _d['L0_attn_hidden_states']
    _d['L0_attn_hidden_states'] = jax.random.normal(jax.random.fold_in(jax.random.key(seed), 1), (8, 1024, 256), dtype=_x0.dtype)
    del _x0
    return _d

def reference(L0_attn_hidden_states, L0_attn_w_in, L0_attn_w_conv, L0_attn_w_xproj, L0_attn_w_dt, L0_attn_b_dt, L0_attn_A_log, L0_attn_D, L0_attn_w_out, L0_ffn_W_qkv, L0_ffn_b_qkv, L0_ffn_W_gate, L0_ffn_b_gate, L0_ffn_W_experts, L0_ffn_b_experts):

    def _L0_attn_ref(hidden_states, w_in, w_conv, w_xproj, w_dt, b_dt, A_log, D, w_out):
        import jax, jax.numpy as jnp
        import numpy as np
        from functools import partial
        B_, L_, H_, DIN_, K_, N_, R_ = (2, 512, 256, 512, 4, 16, 64)

        def _selective_scan(x, delta, A, Bm, Cm, D):
            dA = jnp.exp(jnp.einsum('bld,dn->bldn', delta, A))
            dBx = jnp.einsum('bld,bln->bldn', delta * x, Bm)
            b, l, d, n = dA.shape

            def step(z, inp):
                dA_t, dBx_t, c_t = inp
                z = dA_t * z + dBx_t
                y = jnp.einsum('bdn,bn->bd', z, c_t)
                return (z, y)
            z0 = jnp.zeros((b, d, n), x.dtype)
            _, ys = jax.lax.scan(step, z0, (jnp.moveaxis(dA, 1, 0), jnp.moveaxis(dBx, 1, 0), jnp.moveaxis(Cm, 1, 0)))
            y = jnp.moveaxis(ys, 0, 1)
            return y + x * D
        b, l, h = hidden_states.shape
        d_in, n = A_log.shape
        hs_res = hidden_states @ w_in.T
        hs, res = (hs_res[..., :d_in], hs_res[..., d_in:])
        xc = jnp.moveaxis(hs, 1, 2)
        xc = jax.lax.conv_general_dilated(xc, w_conv, window_strides=(1,), padding=[(K_ - 1, 0)], dimension_numbers=('NCH', 'OIH', 'NCH'), feature_group_count=d_in)
        hs = jax.nn.silu(jnp.moveaxis(xc, 1, 2))
        A = -jnp.exp(A_log)
        x_dbl = hs @ w_xproj.T
        dt, Bm, Cm = (x_dbl[..., :R_], x_dbl[..., R_:R_ + n], x_dbl[..., R_ + n:])
        delta = jax.nn.softplus(dt @ w_dt.T + b_dt)
        y = _selective_scan(hs, delta, A, Bm, Cm, D)
        y = y * jax.nn.silu(res)
        return y @ w_out.T

    def _L0_ffn_ref(x, W_qkv, b_qkv, W_gate, b_gate, W_experts, b_experts):
        import jax, jax.numpy as jnp
        import numpy as np
        NUM_HEADS = 16
        TOP_K = 2
        B, S, D = x.shape
        H = NUM_HEADS
        hd = D // H
        E = W_gate.shape[-1]
        qkv = (x @ W_qkv + b_qkv).reshape(B, S, 3, H, hd)
        q, k, v = (qkv[:, :, 0], qkv[:, :, 1], qkv[:, :, 2])
        attn = jnp.einsum('bqhd,bkhd->bhqk', q, k) / jnp.sqrt(jnp.asarray(hd, x.dtype))
        attn = jax.nn.softmax(attn, axis=-1)
        attn_out = jnp.einsum('bhqk,bkhd->bqhd', attn, v).reshape(B, S, D)
        gate = jax.nn.softmax(x @ W_gate + b_gate, axis=-1)
        top_g, top_i = jax.lax.top_k(gate, TOP_K)
        combine = jnp.sum(jax.nn.one_hot(top_i, E, dtype=x.dtype) * top_g[..., None], axis=2)
        expert_out = jnp.einsum('bsd,edf->bsef', x, W_experts) + b_experts
        moe_out = jnp.einsum('bsef,bse->bsf', expert_out, combine)
        return attn_out + moe_out
    x = L0_attn_hidden_states
    x = _layernorm(x + _L0_attn_ref(x, L0_attn_w_in, L0_attn_w_conv, L0_attn_w_xproj, L0_attn_w_dt, L0_attn_b_dt, L0_attn_A_log, L0_attn_D, L0_attn_w_out), axis=-1)
    x = _layernorm(x + _L0_ffn_ref(x, L0_ffn_W_qkv, L0_ffn_b_qkv, L0_ffn_W_gate, L0_ffn_b_gate, L0_ffn_W_experts, L0_ffn_b_experts), axis=-1)
    return x

_drawn_inputs = setup_inputs


def setup_inputs(seed=0):
    import zlib

    import numpy as np

    out = dict(_drawn_inputs(seed))
    spreads = {'L0_attn_b_dt': (0.0, 2.0),
     'L0_attn_D': (1.0, 0.6),
     'L0_ffn_b_qkv': (0.0, 0.1),
     'L0_ffn_b_gate': (0.0, 0.1),
     'L0_ffn_b_experts': (0.0, 0.329)}
    factors = {'L0_attn_w_xproj': 8.0,
     'L0_attn_w_dt': 8.0,
     'L0_attn_A_log': 28.819,
     'L0_ffn_W_qkv': 5.679}
    for name, (base, spread) in spreads.items():
        noise = np.random.default_rng([zlib.crc32(name.encode()), seed]).standard_normal(out[name].shape)
        drawn = base * np.exp(spread * noise) if base else spread * noise
        out[name] = jnp.asarray(drawn.astype(out[name].dtype))
    for name, factor in factors.items():
        out[name] = (out[name] * factor).astype(out[name].dtype)
    return out
```

```python
from contextlib import ExitStack

import concourse.bass as bass
from concourse import mybir

F32 = mybir.dt.float32
BF16 = mybir.dt.bfloat16
ALU = mybir.AluOpType
ACT = mybir.ActivationFunctionType
AX = mybir.AxisListType

P = 128
NB = 8
T = 1024
TT = T // P
H = 256
KH = H // P
DIN = 512
M = DIN // P
NS = 16
R = 64
KC = 4
PAD = KC - 1
HALF = 512
HEADS = 16
HD = H // HEADS
E = 8
QR = 6 * HD
QPART = (0, 0, 1, 1, 0, 2)
KPART = (0, 1, 0, 1, 2, 0)
QM = QR + 3
VC = 32
EPS = 1e-5


def ds(start, n):
    return bass.ds(start, n)


def layer_norm_stats(dve, stats, ln, chain, value):
    mean_e, mean_o, dev_e, dev_o = (stats[:, :, i] for i in (1, 4, 2, 5))
    dve.tensor_tensor(ln[:, 0, :], mean_e, mean_o, ALU.add).then_inc(chain, 1)
    dve.tensor_tensor(ln[:, 2, :], mean_e, mean_o, ALU.subtract).then_inc(chain, 1)
    dve.tensor_tensor(ln[:, 1, :], dev_e, dev_o, ALU.add).then_inc(chain, 1)
    dve.wait_ge(chain, value(3))
    dve.scalar_tensor_tensor(out=ln[:, 2, :], in0=ln[:, 2, :], scalar=0.25, in1=ln[:, 2, :],
                             op0=ALU.mult, op1=ALU.mult).then_inc(chain, 1)
    dve.tensor_scalar(ln[:, 0, :], ln[:, 0, :], 0.5, None, ALU.mult).then_inc(chain, 1)
    dve.wait_ge(chain, value(4))
    return dve.scalar_tensor_tensor(out=ln[:, 1, :], in0=ln[:, 1, :], scalar=1.0 / H, in1=ln[:, 2, :],
                                    op0=ALU.mult, op1=ALU.add)


def mamba_phase(nc, d):
    with ExitStack() as ctx:
        def sb(name, shape, dt=F32):
            return ctx.enter_context(nc.sbuf_tensor(name, shape, dt))

        def sem(name):
            return ctx.enter_context(nc.semaphore(name))

        ps = ctx.enter_context(nc.psum_tensor("ps1", [P, 8, HALF], F32))

        def pair(i):
            return ps[:, 2 * i:2 * i + 2, :].rearrange("p a b -> p (a b)")

        w_in = sb("w_in", [P, KH, 2 * DIN])
        w_xp = sb("w_xp", [P, M, R + 2 * NS])
        w_dt = sb("w_dt", [R, DIN])
        w_out = sb("w_out", [P, M, H])
        w_conv = sb("w_conv", [P, M, KC])
        b_dt = sb("b_dt", [P, M])
        d_col = sb("d_col", [P, M])
        a_col = sb("a_col", [P, M, NS])
        ident = sb("ident1", [P, P])
        d_diag = sb("d_diag", [P, M, P])
        row_sel = sb("row_sel", [3 * 2 * NS, 2 * NS, P], BF16)
        one_col = sb("one_col1", [P, 1])
        xT = sb("xT", [P, KH, T])
        x_nat = sb("x_nat", [P, TT, H])
        h_raw = sb("h_raw", [P, M, PAD + T])
        hs = sb("hs", [P, M, T])
        s_res = sb("s_res", [P, M, T])
        dt = sb("dt", [R, T])
        bc_parts = sb("bc_parts", [3 * 2 * NS, T], BF16)
        bc_rest = sb("bc_rest", [2 * NS, T])
        bc_mid = sb("bc_mid", [2 * NS, T], BF16)
        sp_l = sb("sp_l", [P, 2, T])
        delta = sb("delta", [P, M, T])
        u = sb("u", [P, M, T])
        dA = sb("dA", [P, 2, T])
        dBx = sb("dBx", [P, 2, T])
        z = sb("z", [P, 2, T])
        zC = sb("zC", [P, 2, T])
        c_rows = sb("c_rows", [P, 2, T])
        conv, sp_e, sp_d = z, dA, dBx
        yg = u
        res = sb("res1", [P, TT, H])
        stats = sb("stats1", [P, TT, 6])
        ln = sb("ln1", [P, 3, TT])
        eps_col = sb("eps_col1", [P, 1])
        rstd = sb("rstd1", [P, TT])

        s_w = sem("weights_loaded1")
        s_const = sem("constants_ready1")
        s_a = sem("a_exp_done")
        s_x = sem("x_loaded")
        s_in = sem("in_proj_done")
        s_ev = sem("in_proj_taken")
        s_cv = sem("conv_step")
        s_cvd = sem("conv_done")
        s_hs = sem("hs_done")
        s_xp = sem("x_proj_done")
        s_dt = sem("dt_taken")
        s_bcs = sem("bc_split_step")
        s_bc = sem("bc_parts_done")
        s_dtp = sem("dt_proj_done")
        s_abs = sem("abs_done")
        s_relu = sem("relu_done")
        s_exp = sem("exp_done")
        s_ln = sem("log_done")
        s_spc = sem("softplus_step")
        s_u = sem("u_done")
        s_b = sem("b_rows_ready")
        s_c = sem("c_rows_ready")
        s_cs = sem("c_rows_taken")
        s_da = sem("dA_ready")
        s_dbx = sem("dBx_ready")
        s_z = sem("z_ready")
        s_zc = sem("zC_ready")
        s_y = sem("zC_added")
        s_yg = sem("y_gated")
        s_o = sem("out_proj_done")
        s_r = sem("residual_added")
        s_lns = sem("ln1_step")
        s_ve = sem("mean_var_done")
        s_lv = sem("log_var_done")
        s_rs = sem("rstd_done")
        s_x1 = sem("x1_done")
        s_st = sem("x1_stored")

        block = ctx.enter_context(nc.Block())

        @block.sync
        def _(sp):
            for dst, src in ((w_in, d["w_in"]), (w_xp, d["w_xp"]), (w_out, d["w_out"])):
                sp.dma_start(dst[:, :, :], src.rearrange("(k p) n -> p k n", p=P)).then_inc(s_w, 16)
            sp.dma_start(w_dt[:, :], d["w_dt"]).then_inc(s_w, 16)
            for dst, src in ((w_conv, d["w_conv"]), (a_col, d["a_log"]), (row_sel, d["row_sel"])):
                sp.dma_start(dst[:, :, :], src).then_inc(s_w, 16)
            for dst, src in ((b_dt, d["b_dt"]), (d_col, d["d"]), (ident, d["ident"])):
                sp.dma_start(dst[:, :], src).then_inc(s_w, 16)
            sp.sem_inc(s_st, 16)
            with sp.Fori(0, NB) as b:
                sp.wait_ge(s_r, TT * b + 1)
                sp.dma_start(xT[:, :, :], d["xT"][ds(b, 1)].rearrange("o (k p) t -> p (o k) t", p=P)).then_inc(s_x, 16)
                sp.dma_start(x_nat[:, :, :], d["x"][ds(b, 1)].rearrange("o (t p) h -> p (o t) h", p=P)).then_inc(s_x, 16)
                sp.wait_ge(s_x1, TT * (b + 1))
                sp.dma_start(d["x1"][ds(b, 1)].rearrange("o (t p) h -> p (o t) h", p=P), res[:, :, :]).then_inc(s_st, 16)
            sp.wait_ge(s_st, 16 * (NB + 1))

        @block.gpsimd
        def _(pool):
            pool.sem_inc(s_zc, 4)
            pool.memset(h_raw[:, :, 0:PAD], 0.0).then_inc(s_const, 1)
            pool.memset(one_col[:, :], 1.0).then_inc(s_const, 1)
            pool.memset(eps_col[:, :], EPS).then_inc(s_const, 1)
            pool.wait_ge(s_w, 160)
            for m in range(M):
                pool.tensor_scalar(d_diag[:, m, :], ident[:, :], d_col[:, m:m + 1], None, ALU.mult).then_inc(s_const, 1)
            pool.wait_ge(s_a, 1)
            pool.tensor_scalar(a_col[:, :, :], a_col[:, :, :], -1.0, None, ALU.mult).then_inc(s_const, 1)
            with pool.Fori(0, NB) as b:
                for mp in range(M // 2):
                    with pool.Fori(0, NS // 2) as n2:
                        for k in range(2):
                            i = b * (M // 2 * NS) + n2 * 2 + (mp * NS + k)
                            for mi in range(2):
                                pool.wait_ge(s_z, i * 2 + (mi + 3))
                                pool.wait_ge(s_cs, i + 2)
                                pool.wait_ge(s_y, i * 2 + (mi + 1))
                                pool.tensor_tensor(zC[:, mi, :], z[:, mi, :], c_rows[:, k, :], ALU.mult).then_inc(s_zc, 1)

        @block.tensor
        def _(pe):
            pe.sem_inc(s_y, 2)
            pe.wait_ge(s_w, 160)
            pe.wait_ge(s_const, M + 4)

            def rows(i, n):
                for half in range(2):
                    if half == 0:
                        pe.wait_ge(s_dbx, i * 2 + 2)
                    mm = pe.matmul(ps[:, 4 + half, :], sel_of(n), bc_parts[:, half * HALF:(half + 1) * HALF],
                                   start=True, stop=True)
                mm.then_inc(s_b, 1)
                pe.wait_ge(s_cs, i + 1)
                for half in range(2):
                    mm = pe.matmul(ps[:, 6 + half, :], sel_of(n + NS), bc_parts[:, half * HALF:(half + 1) * HALF],
                                   start=True, stop=True)
                mm.then_inc(s_c, 1)

            def sel_of(n):
                return row_sel[:, ds(n, 1), :].rearrange("p o c -> p (o c)")

            def add(i, last):
                for mi in range(2):
                    pe.wait_ge(s_zc, i * 2 + (mi + 5))
                    for half in range(2):
                        mm = pe.matmul(ps[:, 2 * mi + half, :], ident[:, :], zC[:, mi, half * HALF:(half + 1) * HALF],
                                       start=False, stop=last, skip_group_check=True)
                    mm.then_inc(s_y, 1)

            with pe.Fori(0, NB) as b:
                pe.wait_ge(s_x, (b + 1) * 32)
                pe.wait_ge(s_r, b * TT + 1)
                for m in range(2 * M):
                    if m >= M:
                        pe.wait_ge(s_ev, b * (2 * M) + (m - M + 1))
                    for half in range(2):
                        for k in range(KH):
                            mm = pe.matmul(ps[:, 2 * (m % M) + half, :], w_in[:, k, m * P:(m + 1) * P],
                                           xT[:, k, half * HALF:(half + 1) * HALF], start=(k == 0), stop=(k == KH - 1))
                    mm.then_inc(s_in, 1)
                pe.wait_ge(s_ev, (b + 1) * (2 * M))
                for m in range(M):
                    pe.wait_ge(s_hs, b * M + (m + 3))
                    for half in range(2):
                        mm = pe.matmul(ps[0:R + 2 * NS, half, :], w_xp[:, m, :], hs[:, m, half * HALF:(half + 1) * HALF],
                                       start=(m == 0), stop=(m == M - 1))
                mm.then_inc(s_xp, 1)
                pe.wait_ge(s_dt, b + 1)
                for m in range(M):
                    if m == M - 1:
                        pe.wait_ge(s_bc, b + 1)
                    for half in range(2):
                        mm = pe.matmul(ps[:, 2 * ((m + 1) % M) + half, :], w_dt[:, m * P:(m + 1) * P],
                                       dt[:, half * HALF:(half + 1) * HALF], start=True, stop=True)
                    mm.then_inc(s_dtp, 1)
                pe.wait_ge(s_relu, (b + 1) * M)
                for mp in range(M // 2):
                    i0 = b * (M // 2 * NS) + mp * NS
                    if mp:
                        pe.wait_ge(s_yg, b * M + 2 * mp)
                    for mi in range(2):
                        for half in range(2):
                            pe.matmul(ps[:, 2 * mi + half, :], d_diag[:, 2 * mp + mi, :],
                                      hs[:, 2 * mp + mi, half * HALF:(half + 1) * HALF],
                                      start=True, stop=False, skip_group_check=True)
                    rows(i0, 0)
                    with pe.Fori(0, NS // 2 - 1) as n2:
                        for k in range(2):
                            n = n2 * 2 + k
                            rows(i0 + n + 1, n + 1)
                            add(i0 + n, False)
                    rows(i0 + (NS - 1), NS - 1)
                    add(i0 + (NS - 2), False)
                    add(i0 + (NS - 1), True)
                pe.wait_ge(s_yg, (b + 1) * M)
                pe.wait_ge(s_cs, (b + 1) * (M // 2 * NS) + 1)
                for t in range(TT):
                    if t >= 4:
                        pe.wait_ge(s_r, b * TT + (t - 2))
                    for m in range(M):
                        mm = pe.matmul(ps[:, 4 + t % 4, 0:H], yg[:, m, t * P:(t + 1) * P], w_out[:, m, :],
                                       start=(m == 0), stop=(m == M - 1))
                    mm.then_inc(s_o, 1)

        @block.scalar
        def _(act):
            act.sem_inc(s_cs, 1)
            act.sem_inc(s_hs, 2)
            act.wait_ge(s_w, 160)
            act.activation(a_col[:, :, :], a_col[:, :, :], ACT.Exp).then_inc(s_a, 1)
            act.wait_ge(s_const, M + 4)
            with act.Fori(0, NB) as b:
                for m in range(2 * M):
                    act.wait_ge(s_in, b * (2 * M) + (m + 1))
                    if m < M:
                        act.activation(h_raw[:, m, PAD:PAD + T], pair(m), ACT.Copy).then_inc(s_ev, 1)
                    else:
                        act.activation(s_res[:, m - M, :], pair(m - M), ACT.Silu).then_inc(s_ev, 1)
                for m in range(M):
                    act.wait_ge(s_cvd, b * M + (m + 1))
                    act.activation(hs[:, m, :], conv[:, m % 2, :], ACT.Silu).then_inc(s_hs, 1)
                act.wait_ge(s_xp, b + 1)
                act.activation(dt[:, :], pair(0)[0:R, :], ACT.Copy).then_inc(s_dt, 1)
                for m in range(M):
                    act.wait_ge(s_dtp, b * M + (m + 1))
                    act.wait_ge(s_u, b * M + (m + 1))
                    pr = pair((m + 1) % M)
                    act.activation(sp_e[:, m % 2, :], pr, ACT.Abs, bias=b_dt[:, m:m + 1]).then_inc(s_abs, 1)
                    act.activation(delta[:, m, :], pr, ACT.Relu, bias=b_dt[:, m:m + 1]).then_inc(s_relu, 1)
                    act.wait_ge(s_abs, b * M + (m + 1))
                    act.activation(sp_e[:, m % 2, :], sp_e[:, m % 2, :], ACT.Exp, scale=-1.0).then_inc(s_exp, 1)
                    act.wait_ge(s_exp, b * M + (m + 1))
                    act.activation(sp_l[:, m % 2, :], sp_e[:, m % 2, :], ACT.Ln, bias=one_col[:, :]).then_inc(s_ln, 1)
                for mp in range(M // 2):
                    act.wait_ge(s_u, b * M + (M + 2))
                    with act.Fori(0, NS // 2) as n2:
                        for k in range(2):
                            i = b * (M // 2 * NS) + n2 * 2 + (mp * NS + k)
                            for mi in range(2):
                                m = 2 * mp + mi
                                act.wait_ge(s_z, i * 2 + (mi + 1))
                                act.activation(dA[:, mi, :], delta[:, m, :], ACT.Exp,
                                               scale=a_col[:, m, ds(n2 * 2 + k, 1)]).then_inc(s_da, 1)
                                if mi == 0:
                                    act.wait_ge(s_c, i + 1)
                                    act.wait_ge(s_zc, i * 2 + 2)
                                    act.activation(c_rows[:, k, :], pair(3), ACT.Copy).then_inc(s_cs, 1)
                act.wait_ge(s_ve, b + 1)
                act.activation(rstd[:, :], ln[:, 1, :], ACT.Ln, bias=eps_col[:, :]).then_inc(s_lv, 1)
                act.wait_ge(s_lv, b + 1)
                act.activation(rstd[:, :], rstd[:, :], ACT.Exp, scale=-0.5).then_inc(s_rs, 1)

        @block.vector
        def _(dve):
            dve.sem_inc(s_u, 2)
            dve.sem_inc(s_z, 2)
            dve.sem_inc(s_dbx, 2)
            dve.sem_inc(s_r, 1)
            dve.wait_ge(s_w, 160)
            dve.wait_ge(s_const, M + 4)
            with dve.Fori(0, NB) as b:
                for m in range(M):
                    dve.wait_ge(s_ev, b * (2 * M) + (m + 1))
                    dve.wait_ge(s_hs, b * M + (m + 1))
                    out = conv[:, m % 2, :]
                    dve.tensor_scalar(out, h_raw[:, m, 0:T], w_conv[:, m, 0:1], None, ALU.mult).then_inc(s_cv, 1)
                    for j in range(1, KC):
                        dve.wait_ge(s_cv, b * (M * (KC - 1)) + (m * (KC - 1) + j))
                        dve.scalar_tensor_tensor(out=out, in0=h_raw[:, m, j:j + T], scalar=w_conv[:, m, j:j + 1],
                                                 in1=out, op0=ALU.mult, op1=ALU.add)\
                           .then_inc(s_cv if j < KC - 1 else s_cvd, 1)
                dve.wait_ge(s_xp, b + 1)
                bc = pair(0)[R:R + 2 * NS, :]
                q = 2 * NS
                dve.tensor_copy(bc_parts[0:q, :], bc).then_inc(s_bcs, 1)
                dve.wait_ge(s_bcs, b * 3 + 1)
                dve.tensor_tensor(bc_rest[:, :], bc, bc_parts[0:q, :], ALU.subtract).then_inc(s_bcs, 1)
                dve.wait_ge(s_bcs, b * 3 + 2)
                dve.tensor_copy(bc_mid[:, :], bc_rest[:, :]).then_inc(s_bcs, 1)
                dve.wait_ge(s_bcs, b * 3 + 3)
                dve.tensor_copy(bc_parts[q:2 * q, :], bc_mid[:, :])
                dve.tensor_tensor(bc_parts[2 * q:3 * q, :], bc_rest[:, :], bc_mid[:, :], ALU.subtract).then_inc(s_bc, 1)
                for m in range(M):
                    st = (b * M + m) * 4
                    dd = sp_d[:, m % 2, :]
                    dve.wait_ge(s_exp, b * M + (m + 1))
                    dve.tensor_scalar(dd, sp_e[:, m % 2, :], 1.0, -1.0, ALU.add, ALU.add).then_inc(s_spc, 1)
                    dve.wait_ge(s_spc, st + 1)
                    dve.tensor_tensor(dd, sp_e[:, m % 2, :], dd, ALU.subtract).then_inc(s_spc, 1)
                    dve.wait_ge(s_spc, st + 2)
                    dve.wait_ge(s_ln, b * M + (m + 1))
                    dve.tensor_tensor(dd, sp_l[:, m % 2, :], dd, ALU.add).then_inc(s_spc, 1)
                    dve.wait_ge(s_spc, st + 3)
                    dve.wait_ge(s_relu, b * M + (m + 1))
                    dve.tensor_tensor(delta[:, m, :], delta[:, m, :], dd, ALU.add).then_inc(s_spc, 1)
                    dve.wait_ge(s_spc, st + 4)
                    dve.tensor_tensor(u[:, m, :], delta[:, m, :], hs[:, m, :], ALU.mult).then_inc(s_u, 1)
                for mp in range(M // 2):
                    with dve.Fori(0, NS // 2) as n2:
                        for k in range(2):
                            dve.wait_ge(s_u, b * M + (2 * mp + 4))
                            i = b * (M // 2 * NS) + n2 * 2 + (mp * NS + k)
                            dve.wait_ge(s_b, i + 1)
                            for mi in range(2):
                                dve.wait_ge(s_z, i * 2 + (mi + 1))
                                dve.tensor_tensor(dBx[:, mi, :], u[:, 2 * mp + mi, :], pair(2), ALU.mult).then_inc(s_dbx, 1)
                            for mi in range(2):
                                dve.wait_ge(s_dbx, i * 2 + (mi + 3))
                                dve.wait_ge(s_da, i * 2 + (mi + 1))
                                dve.wait_ge(s_zc, i * 2 + (mi + 3))
                                dve.tensor_tensor_scan(z[:, mi, :], dA[:, mi, :], dBx[:, mi, :], 0.0,
                                                       ALU.mult, ALU.add).then_inc(s_z, 1)
                    dve.wait_ge(s_y, b * (M * NS) + ((mp + 1) * 2 * NS + 2))
                    for mi in range(2):
                        dve.tensor_tensor(yg[:, 2 * mp + mi, :], s_res[:, 2 * mp + mi, :], pair(mi), ALU.mult).then_inc(s_yg, 1)
                dve.wait_ge(s_st, (b + 1) * 16)
                for t in range(TT):
                    dve.wait_ge(s_o, b * TT + (t + 1))
                    dve.tensor_tensor(res[:, t, :], x_nat[:, t, :], ps[:, 4 + t % 4, 0:H], ALU.add).then_inc(s_r, 1)
                    dve.wait_ge(s_r, b * TT + (t + 2))
                    dve.bn_stats(stats[:, t, :], res[:, t, :]).then_inc(s_lns, 1)
                dve.wait_ge(s_lns, b * (TT + 5) + TT)
                layer_norm_stats(dve, stats, ln, s_lns, lambda k: b * (TT + 5) + (TT + k)).then_inc(s_ve, 1)
                dve.wait_ge(s_rs, b + 1)
                for t in range(TT):
                    dve.tensor_scalar(res[:, t, :], res[:, t, :], ln[:, 0, t:t + 1], rstd[:, t:t + 1],
                                      ALU.subtract, ALU.mult).then_inc(s_x1, 1)


def attention_phase(nc, d):
    with ExitStack() as ctx:
        def sb(name, shape, dt=F32):
            return ctx.enter_context(nc.sbuf_tensor(name, shape, dt))

        def sem(name):
            return ctx.enter_context(nc.semaphore(name))

        ps = ctx.enter_context(nc.psum_tensor("ps2", [P, 8, HALF], F32))

        def pair(i):
            return ps[:, 2 * i:2 * i + 2, :].rearrange("p a b -> p (a b)")

        GV = H + E
        w_qk = sb("w_qk", [P, KH, 2 * H])
        w_vg = sb("w_vg", [P, KH, GV])
        w_e = sb("w_e", [P, KH, E * H])
        b_e = sb("b_e", [E, H])
        b_qk = sb("b_qk", [P, 2 * KH])
        b_vg = sb("b_vg", [P, GV])
        ident = sb("ident2", [P, P])
        fold = sb("fold", [P, VC])
        low = sb("low", [P, E, E])
        eps_col = sb("eps_col2", [P, 1])
        acc = sb("acc", [P, TT, H])
        x1T = sb("x1T", [P, KH, T])
        qk_f = sb("qk_f", [P, 2, T])
        qk_parts = sb("qk_parts", [P, 3, 2 * KH, T], BF16)
        q_st = sb("q_st", [QM, HEADS, T], BF16)
        k_st = sb("k_st", [QM, HEADS, T], BF16)
        v_aug = sb("v_aug", [P, TT, HEADS, VC])
        v_h = sb("v_h", [P, TT, VC])
        gate = sb("gate", [P, TT, E])
        g_one = sb("g_one", [P, 3, TT])
        g_cmp = sb("g_cmp", [P, 2, TT, E, E])
        comb = sb("comb", [P, TT, E])
        combT = sb("combT", [E, T])
        half_max = sb("half_max", [P, TT, 2])
        neg_max = sb("neg_max", [P, 2, TT])
        m_bf = sb("m_bf", [P, 2, TT], BF16)
        m_parts = sb("m_parts", [P, 3, TT])
        m_rows = sb("m_rows", [3 * TT, P], BF16)
        probs = sb("probs", [P, TT, T])
        o_sb = sb("o_sb", [P, T])
        r_sum = sb("r_sum", [P, TT, 1])
        att = sb("att", [P, TT, H])
        stats = sb("stats2", [P, TT, 6])
        ln = sb("ln2", [P, 3, TT])
        rstd = sb("rstd2", [P, TT])

        s_w = sem("weights_loaded2")
        s_const = sem("constants_ready2")
        s_x = sem("x1_loaded")
        s_xt = sem("x1_transposed")
        s_xte = sem("x1T_ready")
        s_qk = sem("qk_proj_done")
        s_qf = sem("qk_taken")
        s_sp = sem("qk_split_step")
        s_parts = sem("qk_parts_done")
        s_qst = sem("qk_parts_stored")
        s_stk = sem("stacks_loaded")
        s_v = sem("v_gate_proj_done")
        s_ve = sem("v_gate_taken")
        s_g = sem("gate_step")
        s_gl = sem("gate_logits_shifted")
        s_ge = sem("gate_exp_done")
        s_rk = sem("gate_ranked")
        s_cb = sem("combine_done")
        s_cbt = sem("combine_transposed")
        s_cbe = sem("combT_ready")
        s_ex = sem("expert_pair_done")
        s_ea = sem("expert_pair_added")
        s_es = sem("expert_first_added")
        s_eb = sem("expert_bias_done")
        s_eba = sem("expert_bias_added")
        s_sc = sem("scores_ready")
        s_mx = sem("half_max_done")
        s_ms = sem("max_split_step")
        s_mp = sem("max_parts_done")
        s_mt = sem("max_transposed")
        s_mr = sem("max_rows_ready")
        s_md = sem("max_rows_stacked")
        s_st = sem("scoresT_ready")
        s_p = sem("probs_ready")
        s_vh = sem("v_head_ready")
        s_pv = sem("pv_group_done")
        s_o = sem("o_taken")
        s_ot = sem("o_transposed")
        s_rc = sem("row_sum_inverted")
        s_nm = sem("head_normalised")
        s_at = sem("attention_added")
        s_lns = sem("ln2_step")
        s_mv = sem("mean_var_done2")
        s_lv = sem("log_var_done2")
        s_rs = sem("rstd_done2")
        s_y = sem("out_tile_done")
        s_done = sem("out_stored")

        WEIGHTS = 16 * 9
        CONSTS = 4
        PRE = 2
        block = ctx.enter_context(nc.Block())

        @block.sync
        def _(sp):
            for dst, src in ((w_qk, d["w_qk"]), (w_vg, d["w_vg"]), (w_e, d["w_e"])):
                sp.dma_start(dst[:, :, :], src.rearrange("(k p) n -> p k n", p=P)).then_inc(s_w, 16)
            for dst, src in ((b_e, d["b_e"]), (b_qk, d["b_qk"]), (ident, d["ident"]), (fold, d["fold"]),
                             (b_vg, d["b_vg"].broadcast_to([P, GV]))):
                sp.dma_start(dst[:, :], src).then_inc(s_w, 16)
            sp.dma_start(low[:, :, :], d["low"]).then_inc(s_w, 16)
            sp.sem_inc(s_done, 16)
            sp.sem_inc(s_md, 16)

            def max_rows(b, h):
                sp.wait_ge(s_mr, b * HEADS + h + 2)
                for part in range(3):
                    sp.dma_start(q_st[QR + part:QR + part + 1, ds(h, 1), :].rearrange("p o (c q) -> p (o c) q", q=P),
                                 m_rows[part * TT:(part + 1) * TT, :]).then_inc(s_md, 16)

            with sp.Fori(0, NB) as b:
                sp.wait_ge(s_done, b * 16 + 16)
                sp.dma_start(acc[:, :, :], d["x1"][ds(b, 1)].rearrange("o (t p) h -> p (o t) h", p=P)).then_inc(s_x, 16)
                for mt in range(2 * KH):
                    sp.wait_ge(s_parts, b * (2 * KH) + (mt + 3))
                    sp.dma_start(d["qk"][:, mt * P:(mt + 1) * P, :].rearrange("c p t -> p c t"),
                                 qk_parts[:, :, mt, :]).then_inc(s_qst, 16)
                sp.wait_ge(s_qst, (b + 1) * (16 * 2 * KH))
                for j in range(6):
                    for stack, part, first in ((q_st, QPART[j], 0), (k_st, KPART[j], H)):
                        sp.dma_start(stack[j * HD:(j + 1) * HD, :, :],
                                     d["qk"][part, first:first + H, :].rearrange("(h r) t -> r h t", r=HD)).then_inc(s_stk, 16)
                with sp.Fori(0, HEADS) as h:
                    max_rows(b, h)
                sp.wait_ge(s_y, (b + 1) * TT)
                sp.dma_start(d["out"][ds(b, 1)].rearrange("o (t p) h -> p (o t) h", p=P), att[:, :, :]).then_inc(s_done, 16)
            sp.wait_ge(s_done, (NB + 1) * 16)

        @block.gpsimd
        def _(pool):
            pool.sem_inc(s_pv, 2)
            pool.memset(k_st[QR:QM, :, :], 1.0).then_inc(s_const, 1)
            pool.wait_ge(s_const, 1)
            pool.memset(v_aug[:, :, :, HD:VC], 0.0).then_inc(s_const, 1)
            pool.wait_ge(s_const, 2)
            pool.memset(v_aug[:, :, :, HD:HD + 1], 1.0).then_inc(s_const, 1)
            pool.memset(eps_col[:, :], EPS).then_inc(s_const, 1)
            pool.wait_ge(s_const, CONSTS)
            with pool.Fori(0, NB) as b:
                with pool.Fori(0, HEADS) as h:
                    pool.wait_ge(s_ve, (b + 1) * TT)
                    pool.wait_ge(s_pv, (b * HEADS + h) * 2 + 2)
                    pool.tensor_copy(v_h[:, :, :], v_aug[:, :, ds(h, 1), :].rearrange("p t o c -> p t (o c)")).then_inc(s_vh, 1)

        @block.tensor
        def _(pe):
            pe.wait_ge(s_w, WEIGHTS)
            pe.wait_ge(s_const, CONSTS)

            def head(stack, rows, h, first, n):
                return stack[0:rows, ds(h, 1), first:first + n].rearrange("p o c -> p (o c)")

            def scores(b, h, unit):
                g = b * HEADS + h
                qt, half = unit // 2, unit % 2
                if unit == 0:
                    pe.wait_ge(s_mr, g + 1)
                pe.wait_ge(s_mx, g * (2 * TT) + (unit + 1))
                pe.matmul(ps[:, half, :], head(q_st, QR, h, qt * P, P), head(k_st, QR, h, half * HALF, HALF),
                          start=True, stop=True).then_inc(s_sc, 1)

            def turn_max(b, h):
                pe.wait_ge(s_mp, b * HEADS + h + 1)
                pe.transpose(ps[0:3 * TT, 0, 0:P], m_parts[:, :, :].rearrange("p c t -> p (c t)"), ident[:, :]).then_inc(s_mt, 1)

            def scores_t(b, h, kt):
                g = b * HEADS + h
                if kt == 0:
                    pe.wait_ge(s_md, g * 48 + 64)
                pe.wait_ge(s_p, g * TT + (kt + 1))
                for half in range(2):
                    mm = pe.matmul(ps[:, 2 + 2 * (kt % 2) + half, :], head(k_st, QM, h, kt * P, P),
                                   head(q_st, QM, h, half * HALF, HALF), start=True, stop=True)
                mm.then_inc(s_st, 1)

            def weigh_v(b, h, group):
                g = b * HEADS + h
                pe.wait_ge(s_p, g * TT + (4 * group + 6))
                pe.wait_ge(s_vh, g + 1)
                if group == 0:
                    pe.wait_ge(s_nm, g + 1)
                for half in range(2):
                    for j in range(4):
                        kt = 4 * group + j
                        mm = pe.matmul(ps[VC * j:VC * (j + 1), 6 + half, :], v_h[:, kt, :],
                                       probs[:, kt, half * HALF:(half + 1) * HALF],
                                       start=(group == 0), stop=(group == 1), skip_group_check=True)
                mm.then_inc(s_pv, 1)

            def turn_o(b, h):
                pe.wait_ge(s_o, b * HEADS + h + 1)
                for qt in range(TT):
                    mm = pe.matmul(ps[:, 6, qt * VC:(qt + 1) * VC], o_sb[:, qt * P:(qt + 1) * P], fold[:, :],
                                   start=True, stop=True)
                mm.then_inc(s_ot, 1)

            def step(b, h, before, ahead):
                for kt in range(TT):
                    scores_t(b, h, kt)
                    if ahead:
                        scores(b, h + PRE, 2 * kt)
                        scores(b, h + PRE, 2 * kt + 1)
                    if kt == 1 and before:
                        weigh_v(b, h - 1, 1)
                    if kt == 4 and before:
                        turn_o(b, h - 1)
                    if kt == 6:
                        weigh_v(b, h, 0)
                if ahead:
                    turn_max(b, h + PRE)

            with pe.Fori(0, NB) as b:
                pe.wait_ge(s_x, (b + 1) * 16)
                pe.wait_ge(s_nm, b * HEADS + 1)
                for k in range(KH):
                    for t in range(TT):
                        mm = pe.transpose(ps[:, 2 * k + t // 4, (t % 4) * P:(t % 4 + 1) * P],
                                          acc[:, t, k * P:(k + 1) * P], ident[:, :])
                    mm.then_inc(s_xt, 1)
                pe.wait_ge(s_xte, (b + 1) * KH)
                for mt in range(2 * KH):
                    for half in range(2):
                        for k in range(KH):
                            mm = pe.matmul(ps[:, (4 + 2 * mt) % 8 + half, :], w_qk[:, k, mt * P:(mt + 1) * P],
                                           x1T[:, k, half * HALF:(half + 1) * HALF], start=(k == 0), stop=(k == KH - 1))
                    mm.then_inc(s_qk, 1)
                for t in range(TT):
                    if t % 2 == 0 and t < 4:
                        pe.wait_ge(s_qf, b * (2 * KH) + (t // 2 + 1))
                    if t >= 4:
                        pe.wait_ge(s_ve, b * TT + (t - 3))
                    for k in range(KH):
                        mm = pe.matmul(ps[:, 4 + t % 4, 0:GV], x1T[:, k, t * P:(t + 1) * P], w_vg[:, k, :],
                                       start=(k == 0), stop=(k == KH - 1))
                    mm.then_inc(s_v, 1)
                pe.wait_ge(s_qf, (b + 1) * (2 * KH))
                pe.wait_ge(s_cb, b + 1)
                for t in range(TT):
                    mm = pe.transpose(ps[0:E, t // 4, (t % 4) * P:(t % 4 + 1) * P], comb[:, t, :], ident[:, :])
                mm.then_inc(s_cbt, 1)
                pe.wait_ge(s_ve, (b + 1) * TT)
                pe.wait_ge(s_cbe, b + 1)
                for t in range(TT):
                    for e2 in range(E // 2):
                        pe.wait_ge(s_ea, b * (TT * E // 2) + (t * (E // 2) + e2 + 1))
                        for k in range(KH):
                            mm = pe.matmul(ps[:, 4 + e2, :], x1T[:, k, t * P:(t + 1) * P],
                                           w_e[:, k, e2 * 2 * H:(e2 + 1) * 2 * H], start=(k == 0), stop=(k == KH - 1))
                        mm.then_inc(s_ex, 1)
                    pe.wait_ge(s_eba, b * TT + (t + 1))
                    pe.matmul(ps[:, 2 + t % 2, 0:H], combT[:, t * P:(t + 1) * P], b_e[:, :],
                              start=True, stop=True).then_inc(s_eb, 1)
                pe.wait_ge(s_ea, (b + 1) * (TT * E // 2) + 4)
                pe.wait_ge(s_eba, (b + 1) * TT + 2)
                pe.wait_ge(s_stk, (b + 1) * (12 * 16))
                for h in range(PRE):
                    for unit in range(2 * TT):
                        scores(b, h, unit)
                    turn_max(b, h)
                step(b, 0, False, True)
                with pe.Fori(1, HEADS - PRE) as h:
                    step(b, h, True, True)
                for h in range(HEADS - PRE, HEADS):
                    step(b, h, True, False)
                weigh_v(b, HEADS - 1, 1)
                turn_o(b, HEADS - 1)

        @block.scalar
        def _(act):
            act.sem_inc(s_p, 2)
            act.sem_inc(s_mr, 1)
            act.wait_ge(s_w, WEIGHTS)
            act.wait_ge(s_const, CONSTS)

            def exp_tile(b, h, kt):
                g = b * HEADS + h
                act.wait_ge(s_st, g * TT + (kt + 1))
                act.wait_ge(s_pv, g * 2 + (kt // 4 + 1))
                act.activation(probs[:, kt, :], pair(1 + kt % 2), ACT.Exp, scale=HD ** -0.5).then_inc(s_p, 1)

            def take_o(b, h):
                g = b * HEADS + h
                act.wait_ge(s_pv, g * 2 + 4)
                act.wait_ge(s_ot, g + 1)
                act.activation(o_sb[:, :], pair(3), ACT.Copy).then_inc(s_o, 1)

            def take_max(b, h):
                g = b * HEADS + h
                act.wait_ge(s_mt, g + 1)
                act.wait_ge(s_md, g * 48 + 16)
                act.activation(m_rows[:, :], ps[0:3 * TT, 0, 0:P], ACT.Copy).then_inc(s_mr, 1)

            def step(b, h, before, ahead):
                for kt in range(TT):
                    exp_tile(b, h, kt)
                    if kt == 2 and before:
                        take_o(b, h - 1)
                if ahead:
                    take_max(b, h + PRE)

            with act.Fori(0, NB) as b:
                for k in range(KH):
                    act.wait_ge(s_xt, b * KH + (k + 1))
                    act.activation(x1T[:, k, :], pair(k), ACT.Copy).then_inc(s_xte, 1)
                for mt in range(2 * KH):
                    act.wait_ge(s_qk, b * (2 * KH) + (mt + 1))
                    act.wait_ge(s_parts, b * (2 * KH) + (mt + 1))
                    act.activation(qk_f[:, mt % 2, :], pair((mt + 2) % 4), ACT.Identity, bias=b_qk[:, mt:mt + 1]).then_inc(s_qf, 1)
                act.wait_ge(s_gl, b + 1)
                act.activation(gate[:, :, :], gate[:, :, :], ACT.Exp).then_inc(s_ge, 1)
                act.wait_ge(s_cbt, b + 1)
                act.activation(combT[:, :], pair(0)[0:E, :], ACT.Copy).then_inc(s_cbe, 1)
                for h in range(PRE):
                    take_max(b, h)
                step(b, 0, False, True)
                with act.Fori(1, HEADS - PRE) as h:
                    step(b, h, True, True)
                for h in range(HEADS - PRE, HEADS):
                    step(b, h, True, False)
                take_o(b, HEADS - 1)
                act.wait_ge(s_mv, b + 1)
                act.activation(rstd[:, :], ln[:, 1, :], ACT.Ln, bias=eps_col[:, :]).then_inc(s_lv, 1)
                act.wait_ge(s_lv, b + 1)
                act.activation(rstd[:, :], rstd[:, :], ACT.Exp, scale=-0.5).then_inc(s_rs, 1)

        @block.vector
        def _(dve):
            dve.sem_inc(s_parts, 2)
            dve.sem_inc(s_ea, 4)
            dve.sem_inc(s_eba, 2)
            dve.sem_inc(s_mx, 2)
            dve.sem_inc(s_ot, 1)
            dve.sem_inc(s_nm, 1)
            dve.wait_ge(s_w, WEIGHTS)

            def take_half_max(b, h, unit):
                g = b * HEADS + h
                dve.wait_ge(s_sc, g * (2 * TT) + (unit + 1))
                dve.tensor_reduce(half_max[:, unit // 2, unit % 2:unit % 2 + 1], ps[:, unit % 2, :], AX.X, ALU.max).then_inc(s_mx, 1)

            def split_max(b, h):
                g = b * HEADS + h
                at = g * 4
                dve.wait_ge(s_mx, g * (2 * TT) + (2 * TT + 2))
                dve.tensor_reduce(neg_max[:, 0, :], half_max[:, :, :], AX.X, ALU.max, negate=True).then_inc(s_ms, 1)
                dve.wait_ge(s_ms, at + 1)
                dve.tensor_copy(m_bf[:, 0, :], neg_max[:, 0, :]).then_inc(s_ms, 1)
                dve.wait_ge(s_ms, at + 2)
                dve.wait_ge(s_mr, g + 1)
                dve.tensor_tensor(neg_max[:, 1, :], neg_max[:, 0, :], m_bf[:, 0, :], ALU.subtract).then_inc(s_ms, 1)
                dve.tensor_copy(m_parts[:, 0, :], m_bf[:, 0, :])
                dve.wait_ge(s_ms, at + 3)
                dve.tensor_copy(m_bf[:, 1, :], neg_max[:, 1, :]).then_inc(s_ms, 1)
                dve.wait_ge(s_ms, at + 4)
                dve.tensor_copy(m_parts[:, 1, :], m_bf[:, 1, :])
                dve.tensor_tensor(m_parts[:, 2, :], neg_max[:, 1, :], m_bf[:, 1, :], ALU.subtract).then_inc(s_mp, 1)

            def normalise(b, h):
                g = b * HEADS + h
                o = ps[:, 6, 0:TT * VC].rearrange("p (t c) -> p t c", c=VC)
                dve.wait_ge(s_ot, g + 2)
                dve.reciprocal(r_sum[:, :, :], o[:, :, HD:HD + 1]).then_inc(s_rc, 1)
                dve.wait_ge(s_rc, g + 1)
                dve.tensor_tensor(att[:, :, ds(h * HD, HD)], o[:, :, 0:HD], r_sum[:, :, :].broadcast_to([P, TT, HD]),
                                  ALU.mult).then_inc(s_nm, 1)

            def step(b, h, before, ahead):
                if ahead:
                    for unit in range(2 * TT):
                        take_half_max(b, h + PRE, unit)
                        if unit == 2 * TT - 4 and before:
                            normalise(b, h - 1)
                    split_max(b, h + PRE)
                elif before:
                    normalise(b, h - 1)

            with dve.Fori(0, NB) as b:
                for mt in range(2 * KH):
                    at = b * (2 * KH * 3) + mt * 3
                    f = qk_f[:, mt % 2, :]
                    dve.wait_ge(s_qf, b * (2 * KH) + (mt + 1))
                    dve.tensor_copy(qk_parts[:, 0, mt, :], f).then_inc(s_sp, 1)
                    dve.wait_ge(s_sp, at + 1)
                    dve.tensor_tensor(f, f, qk_parts[:, 0, mt, :], ALU.subtract).then_inc(s_sp, 1)
                    dve.wait_ge(s_sp, at + 2)
                    dve.tensor_copy(qk_parts[:, 1, mt, :], f).then_inc(s_sp, 1)
                    dve.wait_ge(s_sp, at + 3)
                    dve.tensor_tensor(qk_parts[:, 2, mt, :], f, qk_parts[:, 1, mt, :], ALU.subtract).then_inc(s_parts, 1)
                for t in range(TT):
                    dve.wait_ge(s_v, b * TT + (t + 1))
                    dve.wait_ge(s_const, CONSTS)
                    v = ps[:, 4 + t % 4, :]
                    dve.tensor_tensor(v_aug[:, t, :, 0:HD], v[:, 0:H].rearrange("p (h c) -> p h c", c=HD),
                                      b_vg[:, 0:H].rearrange("p (h c) -> p h c", c=HD), ALU.add)
                    dve.tensor_tensor(gate[:, t, :], v[:, H:GV], b_vg[:, H:GV], ALU.add).then_inc(s_ve, 1)
                at = b * 7
                dve.wait_ge(s_ve, (b + 1) * TT)
                dve.tensor_reduce(g_one[:, 0, :], gate[:, :, :], AX.X, ALU.max).then_inc(s_g, 1)
                dve.wait_ge(s_g, at + 1)
                dve.tensor_tensor(gate[:, :, :], gate[:, :, :], g_one[:, 0, :].unsqueeze(2).broadcast_to([P, TT, E]),
                                  ALU.subtract).then_inc(s_gl, 1)
                dve.wait_ge(s_ge, b + 1)
                dve.tensor_reduce(g_one[:, 1, :], gate[:, :, :], AX.X, ALU.add).then_inc(s_g, 1)
                dve.wait_ge(s_g, at + 2)
                dve.reciprocal(g_one[:, 2, :], g_one[:, 1, :]).then_inc(s_g, 1)
                dve.wait_ge(s_g, at + 3)
                dve.tensor_tensor(gate[:, :, :], gate[:, :, :], g_one[:, 2, :].unsqueeze(2).broadcast_to([P, TT, E]),
                                  ALU.mult).then_inc(s_g, 1)
                dve.wait_ge(s_g, at + 4)
                other = gate[:, :, :].unsqueeze(2).broadcast_to([P, TT, E, E])
                own = gate[:, :, :].unsqueeze(3).broadcast_to([P, TT, E, E])
                dve.tensor_tensor(g_cmp[:, 0, :, :, :], other, own, ALU.is_equal).then_inc(s_g, 1)
                dve.tensor_tensor(g_cmp[:, 1, :, :, :], other, own, ALU.is_gt)
                dve.wait_ge(s_g, at + 5)
                dve.tensor_tensor(g_cmp[:, 0, :, :, :], g_cmp[:, 0, :, :, :],
                                  low[:, :, :].unsqueeze(1).broadcast_to([P, TT, E, E]), ALU.mult).then_inc(s_g, 1)
                dve.wait_ge(s_g, at + 6)
                dve.tensor_tensor(g_cmp[:, 0, :, :, :], g_cmp[:, 0, :, :, :], g_cmp[:, 1, :, :, :], ALU.add).then_inc(s_g, 1)
                dve.wait_ge(s_g, at + 7)
                dve.tensor_reduce(g_cmp[:, 1, :, :, 0], g_cmp[:, 0, :, :, :], AX.X, ALU.add).then_inc(s_rk, 1)
                dve.wait_ge(s_rk, b + 1)
                dve.scalar_tensor_tensor(out=comb[:, :, :], in0=g_cmp[:, 1, :, :, 0], scalar=1.5, in1=gate[:, :, :],
                                         op0=ALU.is_lt, op1=ALU.mult).then_inc(s_cb, 1)
                dve.wait_ge(s_cb, b + 1)
                for t in range(TT):
                    for e in range(E):
                        unit = b * (TT * E // 2) + (t * (E // 2) + e // 2)
                        if e % 2 == 0:
                            dve.wait_ge(s_ex, unit + 1)
                            if e:
                                dve.wait_ge(s_ea, unit + 4)
                        else:
                            dve.wait_ge(s_es, unit + 1)
                        dve.scalar_tensor_tensor(out=acc[:, t, :], in0=ps[:, 4 + e // 2, (e % 2) * H:(e % 2 + 1) * H],
                                                 scalar=comb[:, t, e:e + 1], in1=acc[:, t, :], op0=ALU.mult, op1=ALU.add)\
                           .then_inc(s_ea if e % 2 else s_es, 1)
                    dve.wait_ge(s_eb, b * TT + (t + 1))
                    dve.wait_ge(s_ea, b * (TT * E // 2) + ((t + 1) * (E // 2) + 4))
                    dve.tensor_tensor(acc[:, t, :], acc[:, t, :], ps[:, 2 + t % 2, 0:H], ALU.add).then_inc(s_eba, 1)
                dve.wait_ge(s_done, (b + 1) * 16)
                for h in range(PRE):
                    for unit in range(2 * TT):
                        take_half_max(b, h, unit)
                    split_max(b, h)
                step(b, 0, False, True)
                with dve.Fori(1, HEADS - PRE) as h:
                    step(b, h, True, True)
                for h in range(HEADS - PRE, HEADS):
                    step(b, h, True, False)
                normalise(b, HEADS - 1)
                dve.wait_ge(s_nm, (b + 1) * HEADS + 1)
                dve.wait_ge(s_eba, (b + 1) * TT + 2)
                for t in range(TT):
                    dve.tensor_tensor(acc[:, t, :], acc[:, t, :], att[:, t, :], ALU.add).then_inc(s_at, 1)
                for t in range(TT):
                    dve.wait_ge(s_at, b * TT + (t + 1))
                    dve.bn_stats(stats[:, t, :], acc[:, t, :]).then_inc(s_lns, 1)
                dve.wait_ge(s_lns, b * (TT + 5) + TT)
                layer_norm_stats(dve, stats, ln, s_lns, lambda k: b * (TT + 5) + (TT + k)).then_inc(s_mv, 1)
                dve.wait_ge(s_rs, b + 1)
                for t in range(TT):
                    dve.tensor_scalar(att[:, t, :], acc[:, t, :], ln[:, 0, t:t + 1], rstd[:, t:t + 1],
                                      ALU.subtract, ALU.mult).then_inc(s_y, 1)



def build(nc, d):
    mamba_phase(nc, d)
    attention_phase(nc, d)


def kernel(**inputs):
    import ml_dtypes
    import numpy as np
    import concourse.bacc as bacc
    from concourse.bass_utils import run_bass_kernel_spmd

    a = {k: np.asarray(v) for k, v in inputs.items()}
    x = a["L0_attn_hidden_states"]

    def per_channel(v):
        v = v.reshape((M, P) + v.shape[1:])
        return np.moveaxis(v, 0, 1)

    qkv, bq = a["L0_ffn_W_qkv"], a["L0_ffn_b_qkv"]
    row_sel = np.zeros((3, 2 * NS, 2 * NS, P), np.float32)
    for n in range(2 * NS):
        row_sel[:, n, n, :] = 1.0
    fold = np.zeros((P, VC), np.float32)
    fold[np.arange(P), np.arange(P) % VC] = 1.0
    low = np.broadcast_to(np.tril(np.ones((E, E), np.float32), -1), (P, E, E))
    arrays = {
        "x": x, "xT": x.transpose(0, 2, 1),
        "w_in": a["L0_attn_w_in"].T, "w_xp": a["L0_attn_w_xproj"].T, "w_dt": a["L0_attn_w_dt"].T,
        "w_out": a["L0_attn_w_out"].T, "w_conv": per_channel(a["L0_attn_w_conv"][:, 0, :]),
        "b_dt": per_channel(a["L0_attn_b_dt"]), "d": per_channel(a["L0_attn_D"]),
        "a_log": per_channel(a["L0_attn_A_log"]),
        "ident": np.eye(P, dtype=np.float32), "row_sel": row_sel.reshape(3 * 2 * NS, 2 * NS, P).astype(ml_dtypes.bfloat16),
        "w_qk": qkv[:, 0:2 * H], "w_vg": np.concatenate([qkv[:, 2 * H:], a["L0_ffn_W_gate"]], axis=1),
        "b_qk": bq[0:2 * H].reshape(2 * KH, P).T, "b_vg": np.concatenate([bq[2 * H:], a["L0_ffn_b_gate"]])[None, :],
        "w_e": a["L0_ffn_W_experts"].transpose(1, 0, 2).reshape(H, E * H), "b_e": a["L0_ffn_b_experts"],
        "fold": fold, "low": low,
    }
    nc = bacc.Bacc("TRN2", target_bir_lowering=False, num_devices=1)
    maps, d = {}, {}
    for name, v in arrays.items():
        v = np.ascontiguousarray(v)
        maps["in_" + name] = v
        d[name] = nc.dram_tensor("in_" + name, v.shape, mybir.dt.from_np(v.dtype), kind="ExternalInput").ap()
    d["out"] = nc.dram_tensor("out", (NB, T, H), F32, kind="ExternalOutput").ap()
    d["x1"] = nc.dram_tensor("x1_scratch", (NB, T, H), F32, kind="Internal").ap()
    d["qk"] = nc.dram_tensor("qk_scratch", (3, 2 * KH * P, T), BF16, kind="Internal").ap()
    build(nc, d)
    r = run_bass_kernel_spmd(nc, [maps], core_ids=[0])
    return r.results[0]["out"]
```

```python
from contextlib import ExitStack

import concourse.bass as bass
from concourse import mybir

F32 = mybir.dt.float32
BF16 = mybir.dt.bfloat16
ALU = mybir.AluOpType
ACT = mybir.ActivationFunctionType
AX = mybir.AxisListType

P = 128
NB = 8
T = 1024
TT = T // P
H = 256
KH = H // P
DIN = 512
M = DIN // P
NS = 16
R = 64
KC = 4
PAD = KC - 1
HALF = 512
HEADS = 16
HD = H // HEADS
E = 8
QR = 6 * HD
QPART = (0, 0, 1, 1, 0, 2)
KPART = (0, 1, 0, 1, 2, 0)
QM = QR + 3
VC = 32
EPS = 1e-5


def ds(start, n):
    return bass.ds(start, n)


def layer_norm_stats(dve, stats, ln, chain, value):
    mean_e, mean_o, dev_e, dev_o = (stats[:, :, i] for i in (1, 4, 2, 5))
    dve.tensor_tensor(ln[:, 0, :], mean_e, mean_o, ALU.add).then_inc(chain, 1)
    dve.tensor_tensor(ln[:, 2, :], mean_e, mean_o, ALU.subtract).then_inc(chain, 1)
    dve.tensor_tensor(ln[:, 1, :], dev_e, dev_o, ALU.add).then_inc(chain, 1)
    dve.wait_ge(chain, value(3))
    dve.scalar_tensor_tensor(out=ln[:, 2, :], in0=ln[:, 2, :], scalar=0.25, in1=ln[:, 2, :],
                             op0=ALU.mult, op1=ALU.mult).then_inc(chain, 1)
    dve.tensor_scalar(ln[:, 0, :], ln[:, 0, :], 0.5, None, ALU.mult).then_inc(chain, 1)
    dve.wait_ge(chain, value(4))
    return dve.scalar_tensor_tensor(out=ln[:, 1, :], in0=ln[:, 1, :], scalar=1.0 / H, in1=ln[:, 2, :],
                                    op0=ALU.mult, op1=ALU.add)


def mamba_phase(nc, d):
    with ExitStack() as ctx:
        def sb(name, shape, dt=F32):
            return ctx.enter_context(nc.sbuf_tensor(name, shape, dt))

        def sem(name):
            return ctx.enter_context(nc.semaphore(name))

        ps = ctx.enter_context(nc.psum_tensor("ps1", [P, 8, HALF], F32))

        def pair(i):
            return ps[:, 2 * i:2 * i + 2, :].rearrange("p a b -> p (a b)")

        w_in = sb("w_in", [P, KH, 2 * DIN])
        w_xp = sb("w_xp", [P, M, R + 2 * NS])
        w_dt = sb("w_dt", [R, DIN])
        w_out = sb("w_out", [P, M, H])
        w_conv = sb("w_conv", [P, M, KC])
        b_dt = sb("b_dt", [P, M])
        d_col = sb("d_col", [P, M])
        a_col = sb("a_col", [P, M, NS])
        ident = sb("ident1", [P, P])
        d_diag = sb("d_diag", [P, M, P])
        row_sel = sb("row_sel", [3 * 2 * NS, 2 * NS, P], BF16)
        one_col = sb("one_col1", [P, 1])
        xT = sb("xT", [P, KH, T])
        x_nat = sb("x_nat", [P, TT, H])
        h_raw = sb("h_raw", [P, M, PAD + T])
        hs = sb("hs", [P, M, T])
        s_res = sb("s_res", [P, M, T])
        dt = sb("dt", [R, T])
        bc_parts = sb("bc_parts", [3 * 2 * NS, T], BF16)
        bc_rest = sb("bc_rest", [2 * NS, T])
        bc_mid = sb("bc_mid", [2 * NS, T], BF16)
        sp_x = sb("sp_x", [P, 2, T])
        delta = sb("delta", [P, M, T])
        u = sb("u", [P, M, T])
        dA = sb("dA", [P, 2, T])
        dBx = sb("dBx", [P, 2, T])
        z = sb("z", [P, 2, T])
        zC = sb("zC", [P, 2, T])
        c_rows = sb("c_rows", [P, 2, T])
        conv = (z[:, 0, :], z[:, 1, :], dBx[:, 0, :], dBx[:, 1, :])
        sp_e = (dA[:, 0, :], dA[:, 1, :], zC[:, 0, :], zC[:, 1, :])
        sp_l = (c_rows[:, 0, :], c_rows[:, 1, :], sp_x[:, 0, :], sp_x[:, 1, :])
        sp_d = (dBx[:, 0, :], dBx[:, 1, :], z[:, 0, :], z[:, 1, :])
        yg = u
        res = sb("res1", [P, TT, H])
        stats = sb("stats1", [P, TT, 6])
        ln = sb("ln1", [P, 3, TT])
        eps_col = sb("eps_col1", [P, 1])
        rstd = sb("rstd1", [P, TT])

        s_w = sem("weights_loaded1")
        s_const = sem("constants_ready1")
        s_a = sem("a_exp_done")
        s_xt = sem("xT_loaded")
        s_xn = sem("x_loaded")
        s_in = sem("in_proj_done")
        s_ev = sem("in_proj_taken")
        s_cv = sem("conv_step")
        s_cvd = sem("conv_done")
        s_cvp = sem("conv_step_pool")
        s_cvpd = sem("conv_done_pool")
        s_hs = sem("hs_done")
        s_xp = sem("x_proj_done")
        s_dt = sem("dt_taken")
        s_bcs = sem("bc_split_step")
        s_bc = sem("bc_parts_done")
        s_dtp = sem("dt_proj_done")
        s_abs = sem("abs_done")
        s_relu = sem("relu_done")
        s_exp = sem("exp_done")
        s_ln = sem("log_done")
        s_spc = sem("softplus_step")
        s_dl = sem("delta_done")
        s_u = sem("u_done")
        s_b = sem("b_rows_ready")
        s_c = sem("c_rows_ready")
        s_cs = sem("c_rows_taken")
        s_da = sem("dA_ready")
        s_dbx = sem("dBx_ready")
        s_z = sem("z_ready")
        s_zc = sem("zC_ready")
        s_y = sem("zC_added")
        s_yg = sem("y_gated")
        s_o = sem("out_proj_done")
        s_r = sem("residual_added")
        s_lns = sem("ln1_step")
        s_ve = sem("mean_var_done")
        s_lv = sem("log_var_done")
        s_rs = sem("rstd_done")
        s_x1 = sem("x1_done")
        s_st = sem("x1_stored")

        block = ctx.enter_context(nc.Block())

        UNITS = M // 2 * NS
        CONSTS = M + 4
        WEIGHTS = 16 * 10

        @block.sync
        def _(sp):
            for dst, src in ((w_in, d["w_in"]), (w_xp, d["w_xp"]), (w_out, d["w_out"])):
                sp.dma_start(dst[:, :, :], src.rearrange("(k p) n -> p k n", p=P)).then_inc(s_w, 16)
            sp.dma_start(w_dt[:, :], d["w_dt"]).then_inc(s_w, 16)
            for dst, src in ((w_conv, d["w_conv"]), (a_col, d["a_log"]), (row_sel, d["row_sel"])):
                sp.dma_start(dst[:, :, :], src).then_inc(s_w, 16)
            for dst, src in ((b_dt, d["b_dt"]), (d_col, d["d"]), (ident, d["ident"])):
                sp.dma_start(dst[:, :], src).then_inc(s_w, 16)
            sp.sem_inc(s_st, 16)

            def load_xT(b):
                sp.dma_start(xT[:, :, :], d["xT"][ds(b, 1)].rearrange("o (k p) t -> p (o k) t", p=P)).then_inc(s_xt, 16)

            def load_x(b):
                sp.dma_start(x_nat[:, :, :], d["x"][ds(b, 1)].rearrange("o (t p) h -> p (o t) h", p=P)).then_inc(s_xn, 16)

            def store_x1(b):
                sp.wait_ge(s_x1, (b + 1) * TT)
                sp.dma_start(d["x1"][ds(b, 1)].rearrange("o (t p) h -> p (o t) h", p=P), res[:, :, :]).then_inc(s_st, 16)

            load_xT(0)
            load_x(0)
            with sp.Fori(0, NB - 1) as b:
                sp.wait_ge(s_in, (b + 1) * (2 * M))
                load_xT(b + 1)
                sp.wait_ge(s_r, (b + 1) * TT + 1)
                load_x(b + 1)
                store_x1(b)
            store_x1(NB - 1)
            sp.wait_ge(s_st, (NB + 1) * 16)

        @block.gpsimd
        def _(pool):
            pool.sem_inc(s_zc, 4)
            pool.memset(h_raw[:, :, 0:PAD], 0.0).then_inc(s_const, 1)
            pool.memset(one_col[:, :], 1.0).then_inc(s_const, 1)
            pool.memset(eps_col[:, :], EPS).then_inc(s_const, 1)
            pool.wait_ge(s_w, WEIGHTS)
            for m in range(M):
                pool.tensor_scalar(d_diag[:, m, :], ident[:, :], d_col[:, m:m + 1], None, ALU.mult).then_inc(s_const, 1)
            pool.wait_ge(s_a, 1)
            pool.tensor_scalar(a_col[:, :, :], a_col[:, :, :], -1.0, None, ALU.mult).then_inc(s_const, 1)

            def conv_pool(b):
                m = M - 1
                at = b * (2 * KC - 3)
                pool.wait_ge(s_ev, b * (2 * M) + (m + 1))
                for j in range(KC):
                    tap = sp_x[:, j % 2, :] if j else conv[m]
                    weight = w_conv[:, m, j:j + 1].broadcast_to([P, T])
                    mult = pool.tensor_tensor(tap, h_raw[:, m, j:j + T], weight, ALU.mult)
                    if j:
                        mult.then_inc(s_cvp, 1)
                        pool.wait_ge(s_cvp, at + (2 * j - 1))
                        pool.tensor_tensor(conv[m], conv[m], tap, ALU.add).then_inc(s_cvp if j < KC - 1 else s_cvpd, 1)
                        if j < KC - 1:
                            pool.wait_ge(s_cvp, at + 2 * j)

            def batch(b, last):
                for m in range(M):
                    pool.wait_ge(s_dl, b * M + (m + 1))
                    pool.tensor_tensor(u[:, m, :], delta[:, m, :], hs[:, m, :], ALU.mult).then_inc(s_u, 1)
                for mp in range(M // 2):
                    with pool.Fori(0, NS // 2) as n2:
                        for k in range(2):
                            i = b * UNITS + n2 * 2 + (mp * NS + k)
                            for mi in range(2):
                                pool.wait_ge(s_z, i * 2 + (mi + 3))
                                pool.wait_ge(s_cs, i + 2)
                                pool.wait_ge(s_y, i * 2 + (mi + 1))
                                pool.tensor_tensor(zC[:, mi, :], z[:, mi, :], c_rows[:, k, :], ALU.mult).then_inc(s_zc, 1)
                if not last:
                    conv_pool(b + 1)

            conv_pool(0)
            with pool.Fori(0, NB - 1) as b:
                batch(b, False)
            batch(NB - 1, True)

        @block.tensor
        def _(pe):
            pe.sem_inc(s_y, 2)
            pe.wait_ge(s_w, WEIGHTS)
            pe.wait_ge(s_const, CONSTS)

            def sel_of(n):
                return row_sel[:, ds(n, 1), :].rearrange("p o c -> p (o c)")

            def rows(i, n):
                pe.wait_ge(s_dbx, i * 2 + 2)
                for half in range(2):
                    mm = pe.matmul(ps[:, 4 + half, :], sel_of(n), bc_parts[:, half * HALF:(half + 1) * HALF],
                                   start=True, stop=True)
                mm.then_inc(s_b, 1)
                pe.wait_ge(s_cs, i + 1)
                for half in range(2):
                    mm = pe.matmul(ps[:, 6 + half, :], sel_of(n + NS), bc_parts[:, half * HALF:(half + 1) * HALF],
                                   start=True, stop=True)
                mm.then_inc(s_c, 1)

            def add(i, mi, last=False):
                pe.wait_ge(s_zc, i * 2 + (mi + 5))
                for half in range(2):
                    mm = pe.matmul(ps[:, 2 * mi + half, :], ident[:, :], zC[:, mi, half * HALF:(half + 1) * HALF],
                                   start=False, stop=last, skip_group_check=True)
                mm.then_inc(s_y, 1)

            def in_proj(m, to):
                for half in range(2):
                    for k in range(KH):
                        mm = pe.matmul(ps[:, 2 * to + half, :], w_in[:, k, m * P:(m + 1) * P],
                                       xT[:, k, half * HALF:(half + 1) * HALF], start=(k == 0), stop=(k == KH - 1))
                mm.then_inc(s_in, 1)

            def in_proj_hs(b):
                pe.wait_ge(s_xt, (b + 1) * 16)
                for m in range(M):
                    in_proj(m, m)

            def batch(b, last):
                pe.wait_ge(s_ev, b * (2 * M) + 3)
                in_proj(M, 2)
                pe.wait_ge(s_ev, b * (2 * M) + 4)
                in_proj(M + 1, 3)
                pe.wait_ge(s_r, b * TT + 1)
                in_proj(M + 2, 0)
                in_proj(M + 3, 1)
                pe.wait_ge(s_ev, b * (2 * M) + (M + 1))
                for m in range(M):
                    pe.wait_ge(s_hs, b * M + (m + 1))
                    for half in range(2):
                        mm = pe.matmul(ps[0:R + 2 * NS, 4 + half, :], w_xp[:, m, :], hs[:, m, half * HALF:(half + 1) * HALF],
                                       start=(m == 0), stop=(m == M - 1))
                mm.then_inc(s_xp, 1)
                pe.wait_ge(s_dt, b + 1)
                pe.wait_ge(s_ev, (b + 1) * (2 * M))
                for m in range(M):
                    if m == M - 1:
                        pe.wait_ge(s_bc, b + 1)
                    for half in range(2):
                        mm = pe.matmul(ps[:, 2 * ((m + 3) % M) + half, :], w_dt[:, m * P:(m + 1) * P],
                                       dt[:, half * HALF:(half + 1) * HALF], start=True, stop=True)
                    mm.then_inc(s_dtp, 1)
                pe.wait_ge(s_relu, (b + 1) * M)
                for mp in range(M // 2):
                    i0 = b * UNITS + mp * NS
                    rows(i0, 0)
                    if mp:
                        pe.wait_ge(s_yg, b * M + 2 * mp)
                    for mi in range(2):
                        for half in range(2):
                            pe.matmul(ps[:, 2 * mi + half, :], d_diag[:, 2 * mp + mi, :],
                                      hs[:, 2 * mp + mi, half * HALF:(half + 1) * HALF],
                                      start=True, stop=False, skip_group_check=True)
                    rows(i0 + 1, 1)
                    with pe.Fori(0, NS // 2 - 1) as n2:
                        for k in range(2):
                            n = n2 * 2 + k
                            add(i0 + n, 0)
                            rows(i0 + n + 2, n + 2)
                            add(i0 + n, 1)
                    for n in (NS - 2, NS - 1):
                        add(i0 + n, 0, n == NS - 1)
                        add(i0 + n, 1, n == NS - 1)
                pe.wait_ge(s_yg, (b + 1) * M)
                if not last:
                    pe.wait_ge(s_cs, (b + 1) * UNITS + 1)
                    in_proj_hs(b + 1)
                    pe.wait_ge(s_ev, (b + 1) * (2 * M) + 2)
                for t in range(TT):
                    if t >= 4:
                        pe.wait_ge(s_r, b * TT + (t - 2))
                    for m in range(M):
                        mm = pe.matmul(ps[:, t % 4, 0:H], yg[:, m, t * P:(t + 1) * P], w_out[:, m, :],
                                       start=(m == 0), stop=(m == M - 1))
                    mm.then_inc(s_o, 1)

            in_proj_hs(0)
            with pe.Fori(0, NB - 1) as b:
                batch(b, False)
            batch(NB - 1, True)

        @block.scalar
        def _(act):
            act.sem_inc(s_cs, 1)
            act.wait_ge(s_w, WEIGHTS)
            act.activation(a_col[:, :, :], a_col[:, :, :], ACT.Exp).then_inc(s_a, 1)
            act.wait_ge(s_const, CONSTS)

            def take_hs(b):
                for m in range(M):
                    act.wait_ge(s_in, b * (2 * M) + (m + 1))
                    act.activation(h_raw[:, m, PAD:PAD + T], pair(m), ACT.Copy).then_inc(s_ev, 1)

            def gate_silu(b, m):
                act.wait_ge(s_in, b * (2 * M) + (M + m + 1))
                act.activation(s_res[:, m, :], pair((m + 2) % M), ACT.Silu).then_inc(s_ev, 1)

            def conv_silu(b, m):
                act.wait_ge(*((s_cvd, b * (M - 1) + (m + 1)) if m < M - 1 else (s_cvpd, b + 1)))
                act.activation(hs[:, m, :], conv[m], ACT.Silu).then_inc(s_hs, 1)

            def batch(b, last):
                gate_silu(b, 0)
                gate_silu(b, 1)
                conv_silu(b, 0)
                conv_silu(b, 1)
                gate_silu(b, 2)
                gate_silu(b, 3)
                conv_silu(b, 2)
                conv_silu(b, 3)
                act.wait_ge(s_xp, b + 1)
                act.activation(dt[:, :], pair(2)[0:R, :], ACT.Copy).then_inc(s_dt, 1)
                for m in range(M):
                    act.wait_ge(s_dtp, b * M + (m + 1))
                    pr = pair((m + 3) % M)
                    act.activation(sp_e[m], pr, ACT.Abs, bias=b_dt[:, m:m + 1]).then_inc(s_abs, 1)
                    act.activation(delta[:, m, :], pr, ACT.Relu, bias=b_dt[:, m:m + 1]).then_inc(s_relu, 1)
                for m in range(M):
                    act.wait_ge(s_abs, b * M + (m + 1))
                    act.activation(sp_e[m], sp_e[m], ACT.Exp, scale=-1.0).then_inc(s_exp, 1)
                for m in range(M):
                    act.wait_ge(s_exp, b * M + (m + 1))
                    act.activation(sp_l[m], sp_e[m], ACT.Ln, bias=one_col[:, :]).then_inc(s_ln, 1)
                for mp in range(M // 2):
                    act.wait_ge(s_dl, b * M + (2 * mp + 2))
                    with act.Fori(0, NS // 2) as n2:
                        for k in range(2):
                            i = b * UNITS + n2 * 2 + (mp * NS + k)
                            for mi in range(2):
                                m = 2 * mp + mi
                                act.wait_ge(s_z, i * 2 + (mi + 1))
                                act.activation(dA[:, mi, :], delta[:, m, :], ACT.Exp,
                                               scale=a_col[:, m, ds(n2 * 2 + k, 1)]).then_inc(s_da, 1)
                                if mi == 0:
                                    act.wait_ge(s_c, i + 1)
                                    act.wait_ge(s_zc, i * 2 + 2)
                                    act.activation(c_rows[:, k, :], pair(3), ACT.Copy).then_inc(s_cs, 1)
                if not last:
                    take_hs(b + 1)
                act.wait_ge(s_ve, b + 1)
                act.activation(rstd[:, :], ln[:, 1, :], ACT.Ln, bias=eps_col[:, :]).then_inc(s_lv, 1)
                act.wait_ge(s_lv, b + 1)
                act.activation(rstd[:, :], rstd[:, :], ACT.Exp, scale=-0.5).then_inc(s_rs, 1)

            take_hs(0)
            with act.Fori(0, NB - 1) as b:
                batch(b, False)
            batch(NB - 1, True)

        @block.vector
        def _(dve):
            dve.sem_inc(s_z, 2)
            dve.sem_inc(s_dbx, 2)
            dve.sem_inc(s_r, 1)
            dve.wait_ge(s_w, WEIGHTS)
            dve.wait_ge(s_const, CONSTS)

            def conv_dve(b):
                for m in range(M - 1):
                    dve.wait_ge(s_ev, b * (2 * M) + (m + 1))
                    dve.tensor_scalar(conv[m], h_raw[:, m, 0:T], w_conv[:, m, 0:1], None, ALU.mult).then_inc(s_cv, 1)
                    for j in range(1, KC):
                        dve.wait_ge(s_cv, b * ((M - 1) * (KC - 1)) + (m * (KC - 1) + j))
                        dve.scalar_tensor_tensor(out=conv[m], in0=h_raw[:, m, j:j + T], scalar=w_conv[:, m, j:j + 1],
                                                 in1=conv[m], op0=ALU.mult, op1=ALU.add)\
                           .then_inc(s_cv if j < KC - 1 else s_cvd, 1)

            def split_bc(b):
                dve.wait_ge(s_xp, b + 1)
                bc = pair(2)[R:R + 2 * NS, :]
                q = 2 * NS
                dve.tensor_copy(bc_parts[0:q, :], bc).then_inc(s_bcs, 1)
                dve.wait_ge(s_bcs, b * 3 + 1)
                dve.tensor_tensor(bc_rest[:, :], bc, bc_parts[0:q, :], ALU.subtract).then_inc(s_bcs, 1)
                dve.wait_ge(s_bcs, b * 3 + 2)
                dve.tensor_copy(bc_mid[:, :], bc_rest[:, :]).then_inc(s_bcs, 1)
                dve.wait_ge(s_bcs, b * 3 + 3)
                dve.tensor_copy(bc_parts[q:2 * q, :], bc_mid[:, :])
                dve.tensor_tensor(bc_parts[2 * q:3 * q, :], bc_rest[:, :], bc_mid[:, :], ALU.subtract).then_inc(s_bc, 1)

            def softplus_end(b):
                st = b * (3 * M)
                for m in range(M):
                    dve.wait_ge(s_exp, b * M + (m + 1))
                    dve.tensor_scalar(sp_d[m], sp_e[m], 1.0, -1.0, ALU.add, ALU.add).then_inc(s_spc, 1)
                for m in range(M):
                    dve.wait_ge(s_spc, st + (m + 1))
                    dve.tensor_tensor(sp_d[m], sp_e[m], sp_d[m], ALU.subtract).then_inc(s_spc, 1)
                for m in range(M):
                    dve.wait_ge(s_spc, st + (M + m + 1))
                    dve.wait_ge(s_ln, b * M + (m + 1))
                    dve.tensor_tensor(sp_d[m], sp_l[m], sp_d[m], ALU.add).then_inc(s_spc, 1)
                    dve.wait_ge(s_spc, st + (2 * M + m + 1))
                    dve.wait_ge(s_relu, b * M + (m + 1))
                    dve.tensor_tensor(delta[:, m, :], delta[:, m, :], sp_d[m], ALU.add).then_inc(s_dl, 1)

            def batch(b, last):
                split_bc(b)
                softplus_end(b)
                for mp in range(M // 2):
                    with dve.Fori(0, NS // 2) as n2:
                        for k in range(2):
                            i = b * UNITS + n2 * 2 + (mp * NS + k)
                            dve.wait_ge(s_u, b * M + (2 * mp + 2))
                            dve.wait_ge(s_b, i + 1)
                            for mi in range(2):
                                dve.wait_ge(s_z, i * 2 + (mi + 1))
                                dve.tensor_tensor(dBx[:, mi, :], u[:, 2 * mp + mi, :], pair(2), ALU.mult).then_inc(s_dbx, 1)
                            for mi in range(2):
                                dve.wait_ge(s_dbx, i * 2 + (mi + 3))
                                dve.wait_ge(s_da, i * 2 + (mi + 1))
                                dve.wait_ge(s_zc, i * 2 + (mi + 3))
                                dve.tensor_tensor_scan(z[:, mi, :], dA[:, mi, :], dBx[:, mi, :], 0.0,
                                                       ALU.mult, ALU.add).then_inc(s_z, 1)
                    dve.wait_ge(s_y, b * (M * NS) + ((mp + 1) * 2 * NS + 2))
                    for mi in range(2):
                        dve.tensor_tensor(yg[:, 2 * mp + mi, :], s_res[:, 2 * mp + mi, :], pair(mi), ALU.mult).then_inc(s_yg, 1)
                if not last:
                    conv_dve(b + 1)
                dve.wait_ge(s_st, (b + 1) * 16)
                dve.wait_ge(s_xn, (b + 1) * 16)
                for t in range(TT):
                    dve.wait_ge(s_o, b * TT + (t + 1))
                    dve.tensor_tensor(res[:, t, :], x_nat[:, t, :], ps[:, t % 4, 0:H], ALU.add).then_inc(s_r, 1)
                for t in range(TT):
                    dve.wait_ge(s_r, b * TT + (t + 2))
                    dve.bn_stats(stats[:, t, :], res[:, t, :]).then_inc(s_lns, 1)
                dve.wait_ge(s_lns, b * (TT + 5) + TT)
                layer_norm_stats(dve, stats, ln, s_lns, lambda k: b * (TT + 5) + (TT + k)).then_inc(s_ve, 1)
                dve.wait_ge(s_rs, b + 1)
                for t in range(TT):
                    dve.tensor_scalar(res[:, t, :], res[:, t, :], ln[:, 0, t:t + 1], rstd[:, t:t + 1],
                                      ALU.subtract, ALU.mult).then_inc(s_x1, 1)

            conv_dve(0)
            with dve.Fori(0, NB - 1) as b:
                batch(b, False)
            batch(NB - 1, True)


def attention_phase(nc, d):
    with ExitStack() as ctx:
        def sb(name, shape, dt=F32):
            return ctx.enter_context(nc.sbuf_tensor(name, shape, dt))

        def sem(name):
            return ctx.enter_context(nc.semaphore(name))

        ps = ctx.enter_context(nc.psum_tensor("ps2", [P, 8, HALF], F32))

        def pair(i):
            return ps[:, 2 * i:2 * i + 2, :].rearrange("p a b -> p (a b)")

        GV = H + E
        w_qk = sb("w_qk", [P, KH, 2 * H])
        w_vg = sb("w_vg", [P, KH, GV])
        w_e = sb("w_e", [P, KH, E * H])
        b_e = sb("b_e", [E, H])
        b_qk = sb("b_qk", [P, 2 * KH])
        b_vg = sb("b_vg", [P, GV])
        ident = sb("ident2", [P, P])
        fold = sb("fold", [P, VC])
        low = sb("low", [P, E, E])
        eps_col = sb("eps_col2", [P, 1])
        x_in = sb("x_in", [P, TT, H])
        acc = sb("acc", [P, TT, H])
        x1T = sb("x1T", [P, KH, T])
        qk_rest = sb("qk_rest", [P, T])
        qk_parts = sb("qk_parts", [P, 3, 2 * KH, T], BF16)
        q_st = sb("q_st", [QM, HEADS, T], BF16)
        k_st = sb("k_st", [QM, HEADS, T], BF16)
        v_aug = sb("v_aug", [P, TT, HEADS, VC])
        v_h = sb("v_h", [P, TT, VC])
        gate = sb("gate", [P, TT, E])
        g_one = sb("g_one", [P, 3, TT])
        comb = sb("comb", [P, TT, E])
        combT = sb("combT", [E, T])
        neg_max = sb("neg_max", [P, TT])
        m_rest = sb("m_rest", [P, 2, TT])
        m_bf = sb("m_bf", [P, 2, TT], BF16)
        m_parts = sb("m_parts", [P, 3, TT])
        m_rows = sb("m_rows", [3 * TT, P], BF16)
        probs = sb("probs", [P, TT, T])
        g_cmp = probs[:, 0, :].rearrange("p (s t e f) -> p s t e f", s=2, t=TT, e=E)
        o_sb = sb("o_sb", [P, T])
        r_sum = sb("r_sum", [P, TT, 1])
        att = sb("att", [P, TT, H])
        stats = sb("stats2", [P, TT, 6])
        ln = sb("ln2", [P, 3, TT])
        rstd = sb("rstd2", [P, TT])

        s_w = sem("weights_loaded2")
        s_const = sem("constants_ready2")
        s_x = sem("x1_loaded")
        s_xt = sem("x1_transposed")
        s_xte = sem("x1T_ready")
        s_qk = sem("qk_proj_done")
        s_qf = sem("qk_proj_taken")
        s_sp = sem("qk_split_step")
        s_parts = sem("qk_parts_done")
        s_qst = sem("qk_parts_stored")
        s_stk = sem("stacks_loaded")
        s_v = sem("v_gate_proj_done")
        s_ve = sem("v_gate_taken")
        s_g = sem("gate_step")
        s_gl = sem("gate_logits_shifted")
        s_ge = sem("gate_exp_done")
        s_rk = sem("gate_ranked")
        s_cb = sem("combine_done")
        s_cbt = sem("combine_transposed")
        s_cbe = sem("combT_ready")
        s_ex = sem("expert_pair_done")
        s_ea = sem("expert_pair_added")
        s_es = sem("expert_first_added")
        s_eb = sem("expert_bias_done")
        s_eba = sem("expert_bias_added")
        s_sc = sem("scores_ready")
        s_mx = sem("max_done")
        s_ms = sem("max_split_step")
        s_mp = sem("max_parts_done")
        s_mt = sem("max_transposed")
        s_mr = sem("max_rows_ready")
        s_md = sem("max_rows_stacked")
        s_st = sem("scoresT_ready")
        s_p = sem("probs_ready")
        s_vh = sem("v_head_ready")
        s_pv = sem("pv_chunk_done")
        s_o = sem("o_half_taken")
        s_ot = sem("o_transposed")
        s_rc = sem("row_sum_inverted")
        s_nm = sem("head_normalised")
        s_at = sem("attention_added")
        s_lns = sem("ln2_step")
        s_mv = sem("mean_var_done2")
        s_lv = sem("log_var_done2")
        s_rs = sem("rstd_done2")
        s_y = sem("out_tile_done")
        s_done = sem("out_stored")

        WEIGHTS = 16 * 9
        CONSTS = 4
        PRE = 2
        EBANKS = 3
        EU = TT * E // 2
        EARLY = (TT - PRE * TT // (E // 2))
        block = ctx.enter_context(nc.Block())

        @block.sync
        def _(sp):
            for dst, src in ((w_qk, d["w_qk"]), (w_vg, d["w_vg"]), (w_e, d["w_e"])):
                sp.dma_start(dst[:, :, :], src.rearrange("(k p) n -> p k n", p=P)).then_inc(s_w, 16)
            for dst, src in ((b_e, d["b_e"]), (b_qk, d["b_qk"]), (ident, d["ident"]), (fold, d["fold"]),
                             (b_vg, d["b_vg"].broadcast_to([P, GV]))):
                sp.dma_start(dst[:, :], src).then_inc(s_w, 16)
            sp.dma_start(low[:, :, :], d["low"]).then_inc(s_w, 16)
            sp.sem_inc(s_done, 16)
            sp.sem_inc(s_md, 16)

            def load_x(b):
                sp.dma_start(x_in[:, :, :], d["x1"][ds(b, 1)].rearrange("o (t p) h -> p (o t) h", p=P)).then_inc(s_x, 16)

            def store_parts(b):
                for mt in range(2 * KH):
                    sp.wait_ge(s_parts, b * (2 * KH) + (mt + 1))
                    sp.dma_start(d["qk"][:, mt * P:(mt + 1) * P, :].rearrange("c p t -> p c t"),
                                 qk_parts[:, :, mt, :]).then_inc(s_qst, 16)

            def load_stacks(b):
                sp.wait_ge(s_qst, (b + 1) * (16 * 2 * KH))
                for j in range(6):
                    for stack, part, first in ((q_st, QPART[j], 0), (k_st, KPART[j], H)):
                        sp.dma_start(stack[j * HD:(j + 1) * HD, :, :],
                                     d["qk"][part, first:first + H, :].rearrange("(h r) t -> r h t", r=HD)).then_inc(s_stk, 16)

            def max_rows(b, h):
                sp.wait_ge(s_mr, b * HEADS + h + 2)
                for part in range(3):
                    sp.dma_start(q_st[QR + part:QR + part + 1, ds(h, 1), :].rearrange("p o (c q) -> p (o c) q", q=P),
                                 m_rows[part * TT:(part + 1) * TT, :]).then_inc(s_md, 16)

            def store_out(b):
                sp.wait_ge(s_y, (b + 1) * TT)
                sp.dma_start(d["out"][ds(b, 1)].rearrange("o (t p) h -> p (o t) h", p=P), att[:, :, :]).then_inc(s_done, 16)

            load_x(0)
            store_parts(0)
            load_stacks(0)
            with sp.Fori(0, NB - 1) as b:
                max_rows(b, 0)
                sp.wait_ge(s_ea, (b + 1) * EU + EBANKS)
                load_x(b + 1)
                with sp.Fori(1, HEADS) as h:
                    max_rows(b, h)
                store_parts(b + 1)
                sp.wait_ge(s_p, (b + 1) * (HEADS * 2 * TT) + 2)
                load_stacks(b + 1)
                store_out(b)
            with sp.Fori(0, HEADS) as h:
                max_rows(NB - 1, h)
            store_out(NB - 1)
            sp.wait_ge(s_done, (NB + 1) * 16)

        @block.gpsimd
        def _(pool):
            pool.sem_inc(s_pv, 4)
            pool.memset(k_st[QR:QM, :, :], 1.0).then_inc(s_const, 1)
            pool.wait_ge(s_const, 1)
            pool.memset(v_aug[:, :, :, HD:VC], 0.0).then_inc(s_const, 1)
            pool.wait_ge(s_const, 2)
            pool.memset(v_aug[:, :, :, HD:HD + 1], 1.0).then_inc(s_const, 1)
            pool.memset(eps_col[:, :], EPS).then_inc(s_const, 1)
            pool.wait_ge(s_const, CONSTS)
            with pool.Fori(0, NB) as b:
                with pool.Fori(0, HEADS) as h:
                    pool.wait_ge(s_ve, (b + 1) * TT)
                    pool.wait_ge(s_pv, (b * HEADS + h) * 4 + 4)
                    pool.tensor_copy(v_h[:, :, :], v_aug[:, :, ds(h, 1), :].rearrange("p t o c -> p t (o c)")).then_inc(s_vh, 1)

        @block.tensor
        def _(pe):
            pe.wait_ge(s_w, WEIGHTS)
            pe.wait_ge(s_const, CONSTS)

            def head(stack, rows, h, first, n):
                return stack[0:rows, ds(h, 1), first:first + n].rearrange("p o c -> p (o c)")

            def scores(b, h, qt, half):
                g = b * HEADS + h
                if half == 0:
                    pe.wait_ge(s_mx, g * TT + (qt + 1))
                mm = pe.matmul(ps[:, 2 * (qt % 2) + half, :], head(q_st, QR, h, qt * P, P),
                               head(k_st, QR, h, half * HALF, HALF), start=True, stop=True)
                if half == 1:
                    mm.then_inc(s_sc, 1)

            def turn_max(b, h):
                pe.wait_ge(s_mp, b * HEADS + h + 1)
                pe.transpose(ps[0:3 * TT, 7, 0:P], m_parts[:, :, :].rearrange("p c t -> p (c t)"), ident[:, :]).then_inc(s_mt, 1)

            def scores_t(b, h, kt, half):
                g = b * HEADS + h
                if kt == 0 and half == 0:
                    pe.wait_ge(s_md, g * 48 + 64)
                pe.wait_ge(s_p, g * (2 * TT) + (2 * kt + half + 1))
                pe.matmul(ps[:, 4 + half, :], head(k_st, QM, h, kt * P, P),
                          head(q_st, QM, h, half * HALF, HALF), start=True, stop=True).then_inc(s_st, 1)

            def weigh_v(b, h, group, half, turned=False):
                g = b * HEADS + h
                pe.wait_ge(s_p, g * (2 * TT) + (2 * (4 * group + 3) + half + 3))
                if group == 0 and half == 0:
                    pe.wait_ge(s_vh, g + 1)
                    pe.wait_ge(s_nm, g + 1)
                if turned:
                    pe.wait_ge(s_mr, g + 3)
                for j in range(4):
                    kt = 4 * group + j
                    mm = pe.matmul(ps[VC * j:VC * (j + 1), 6 + half, :], v_h[:, kt, :],
                                   probs[:, kt, half * HALF:(half + 1) * HALF],
                                   start=(group == 0), stop=(group == 1), skip_group_check=True)
                mm.then_inc(s_pv, 1)

            def turn_o(b, h, half):
                pe.wait_ge(s_o, (b * HEADS + h) * 2 + (half + 1))
                for qt in range(4 * half, 4 * half + 4):
                    mm = pe.matmul(ps[:, 6, qt * VC:(qt + 1) * VC], o_sb[:, qt * P:(qt + 1) * P], fold[:, :],
                                   start=True, stop=True)
                if half == 1:
                    mm.then_inc(s_ot, 1)

            def turn_x(b, k):
                pe.wait_ge(s_x, (b + 1) * 16)
                pe.wait_ge(s_mx, b * (HEADS * TT) + 2)
                for t in range(TT):
                    mm = pe.transpose(ps[:, 2 * k + t // 4, (t % 4) * P:(t % 4 + 1) * P],
                                      x_in[:, t, k * P:(k + 1) * P], ident[:, :])
                mm.then_inc(s_xt, 1)

            def qk_proj(b, mt, half):
                if mt == 0:
                    pe.wait_ge(s_xte, (b + 1) * KH)
                if mt >= 2:
                    pe.wait_ge(s_qf, b * (2 * KH) + (mt - 1))
                for k in range(KH):
                    mm = pe.matmul(ps[:, 2 * (mt % 2) + half, :], w_qk[:, k, mt * P:(mt + 1) * P],
                                   x1T[:, k, half * HALF:(half + 1) * HALF], start=(k == 0), stop=(k == KH - 1))
                if half == 1:
                    mm.then_inc(s_qk, 1)

            def v_proj(b, t):
                if t < 4:
                    pe.wait_ge(s_qf, b * (2 * KH) + (3 + t // 2))
                else:
                    pe.wait_ge(s_ve, b * TT + (t - 3))
                for k in range(KH):
                    mm = pe.matmul(ps[:, t % 4, 0:GV], x1T[:, k, t * P:(t + 1) * P], w_vg[:, k, :],
                                   start=(k == 0), stop=(k == KH - 1))
                mm.then_inc(s_v, 1)

            def step(b, h, before, ahead, front):
                turned = ahead or h == HEADS - PRE
                for kt in range(TT):
                    for half in range(2):
                        scores_t(b, h, kt, half)
                        if ahead:
                            scores(b, h + PRE, kt, half)
                    if before and kt in (1, 2):
                        weigh_v(b, h - 1, 1, kt - 1)
                    if before and kt in (3, 4):
                        turn_o(b, h - 1, kt - 3)
                    if turned and kt == 4:
                        turn_max(b, h + 1)
                    if kt in (6, 7):
                        weigh_v(b, h, 0, kt - 6, turned and kt == 7)
                    for work, args in front.get(kt, ()):
                        work(b + 1, *args)

            def heads(b, more):
                pe.wait_ge(s_ea, (b + 1) * EU + EBANKS)
                step(b, 0, False, True, {})
                with pe.Fori(1, HEADS - PRE) as h:
                    step(b, h, True, True, {})
                step(b, HEADS - 2, True, False, {} if not more else
                     {0: [(turn_x, (0,))], 1: [(turn_x, (1,))], 3: [(qk_proj, (0, 0))], 4: [(qk_proj, (0, 1))],
                      5: [(qk_proj, (1, 0))], 6: [(qk_proj, (1, 1))]})
                step(b, HEADS - 1, True, False, {} if not more else
                     {0: [(qk_proj, (2, 0))], 1: [(qk_proj, (2, 1))], 2: [(qk_proj, (3, 0))], 3: [(qk_proj, (3, 1))]})
                weigh_v(b, HEADS - 1, 1, 0)
                weigh_v(b, HEADS - 1, 1, 1)
                if more:
                    for t in range(4):
                        v_proj(b + 1, t)
                turn_o(b, HEADS - 1, 0)
                turn_o(b, HEADS - 1, 1)

            def experts(b):
                for t in range(4, TT):
                    v_proj(b, t)
                pe.wait_ge(s_nm, b * HEADS + 1)
                for t in range(TT):
                    for e2 in range(E // 2):
                        u = t * (E // 2) + e2
                        pe.wait_ge(s_ea, b * EU + (u + 1))
                        for k in range(KH):
                            mm = pe.matmul(ps[:, 4 + u % EBANKS, :], x1T[:, k, t * P:(t + 1) * P],
                                           w_e[:, k, e2 * 2 * H:(e2 + 1) * 2 * H], start=(k == 0), stop=(k == KH - 1))
                        mm.then_inc(s_ex, 1)
                        if t >= EARLY:
                            unit = u - EARLY * (E // 2)
                            if unit == 0:
                                pe.wait_ge(s_stk, (b + 1) * (12 * 16))
                                pe.wait_ge(s_eba, (b + 1) * 4)
                            for half in range(2):
                                scores(b, unit // TT, unit % TT, half)
                            if unit == TT + 5:
                                turn_max(b, 0)
                    if t == 0:
                        pe.wait_ge(s_cb, b + 1)
                        pe.wait_ge(s_ve, (b + 1) * TT)
                        for q in range(TT):
                            mm = pe.transpose(ps[0:E, q // 4, (q % 4) * P:(q % 4 + 1) * P], comb[:, q, :], ident[:, :])
                        mm.then_inc(s_cbt, 1)
                    if t == 1:
                        pe.wait_ge(s_cbe, b + 1)
                        for q in range(TT):
                            mm = pe.matmul(ps[:, q // 2, (q % 2) * H:(q % 2 + 1) * H], combT[:, q * P:(q + 1) * P],
                                           b_e[:, :], start=True, stop=True)
                        mm.then_inc(s_eb, 1)

            for k in range(KH):
                turn_x(0, k)
            for mt in range(2 * KH):
                for half in range(2):
                    qk_proj(0, mt, half)
            for t in range(4):
                v_proj(0, t)
            experts(0)
            with pe.Fori(0, NB - 1) as b:
                heads(b, True)
                experts(b + 1)
            heads(NB - 1, False)

        @block.scalar
        def _(act):
            act.sem_inc(s_p, 2)
            act.sem_inc(s_mr, 1)
            act.wait_ge(s_w, WEIGHTS)
            act.wait_ge(s_const, CONSTS)

            def exp_unit(b, h, kt, half):
                g = b * HEADS + h
                act.wait_ge(s_st, g * (2 * TT) + (2 * kt + half + 1))
                act.wait_ge(s_pv, g * 4 + (2 * (kt // 4) + half + 1))
                act.activation(probs[:, kt, half * HALF:(half + 1) * HALF], ps[:, 4 + half, :], ACT.Exp,
                               scale=HD ** -0.5).then_inc(s_p, 1)

            def take_o(b, h, half):
                g = b * HEADS + h
                act.wait_ge(s_pv, g * 4 + (half + 7))
                act.wait_ge(s_ot, g + 1)
                act.activation(o_sb[:, half * HALF:(half + 1) * HALF], ps[:, 6 + half, :], ACT.Copy).then_inc(s_o, 1)

            def take_max(b, h):
                g = b * HEADS + h
                act.wait_ge(s_mt, g + 1)
                act.wait_ge(s_md, g * 48 + 16)
                act.activation(m_rows[:, :], ps[0:3 * TT, 7, 0:P], ACT.Copy).then_inc(s_mr, 1)

            def step(b, h, before, turned):
                for kt in range(TT):
                    for half in range(2):
                        exp_unit(b, h, kt, half)
                        if before and kt in (2, 3) and half == 0:
                            take_o(b, h - 1, kt - 2)
                        if turned and kt == 5 and half == 0:
                            take_max(b, h + 1)

            def heads(b):
                step(b, 0, False, True)
                with act.Fori(1, HEADS - 1) as h:
                    step(b, h, True, True)
                step(b, HEADS - 1, True, False)
                take_o(b, HEADS - 1, 0)
                take_o(b, HEADS - 1, 1)

            def inv_std(b):
                act.wait_ge(s_mv, b + 1)
                act.activation(rstd[:, :], ln[:, 1, :], ACT.Ln, bias=eps_col[:, :]).then_inc(s_lv, 1)
                act.wait_ge(s_lv, b + 1)
                act.activation(rstd[:, :], rstd[:, :], ACT.Exp, scale=-0.5).then_inc(s_rs, 1)

            def gates(b):
                act.wait_ge(s_gl, b + 1)
                act.activation(gate[:, :, :], gate[:, :, :], ACT.Exp).then_inc(s_ge, 1)
                act.wait_ge(s_cbt, b + 1)
                act.activation(combT[:, :], pair(0)[0:E, :], ACT.Copy).then_inc(s_cbe, 1)

            gates(0)
            take_max(0, 0)
            with act.Fori(0, NB - 1) as b:
                heads(b)
                gates(b + 1)
                inv_std(b)
                take_max(b + 1, 0)
            heads(NB - 1)
            inv_std(NB - 1)

        @block.vector
        def _(dve):
            dve.sem_inc(s_ea, EBANKS)
            dve.sem_inc(s_mx, 2)
            dve.sem_inc(s_ot, 1)
            dve.sem_inc(s_nm, 1)
            dve.wait_ge(s_w, WEIGHTS)
            dve.wait_ge(s_const, CONSTS)

            def take_x(b, k):
                dve.wait_ge(s_xt, b * KH + (k + 1))
                dve.tensor_copy(x1T[:, k, :], pair(k)).then_inc(s_xte, 1)

            def split_qk(b, mt):
                at = b * (2 * KH * 2) + mt * 2
                bias = b_qk[:, mt:mt + 1]
                dve.wait_ge(s_qk, b * (2 * KH) + (mt + 1))
                dve.tensor_scalar(qk_parts[:, 0, mt, :], pair(mt % 2), bias, None, ALU.add).then_inc(s_sp, 1)
                dve.wait_ge(s_sp, at + 1)
                dve.scalar_tensor_tensor(out=qk_rest[:, :], in0=pair(mt % 2), scalar=bias, in1=qk_parts[:, 0, mt, :],
                                         op0=ALU.add, op1=ALU.subtract).then_inc(s_qf, 1)
                dve.wait_ge(s_qf, b * (2 * KH) + (mt + 1))
                dve.tensor_copy(qk_parts[:, 1, mt, :], qk_rest[:, :]).then_inc(s_sp, 1)
                dve.wait_ge(s_sp, at + 2)
                dve.tensor_tensor(qk_parts[:, 2, mt, :], qk_rest[:, :], qk_parts[:, 1, mt, :], ALU.subtract).then_inc(s_parts, 1)

            def split_max(b, h, stage):
                g = b * HEADS + h
                at = g * 4
                if stage == 0:
                    dve.wait_ge(s_mx, g * TT + (TT + 2))
                    dve.tensor_copy(m_rest[:, 0, :], neg_max[:, :]).then_inc(s_ms, 1)
                    dve.tensor_copy(m_bf[:, 0, :], neg_max[:, :]).then_inc(s_ms, 1)
                if stage == 1:
                    dve.wait_ge(s_ms, at + 2)
                    dve.tensor_tensor(m_rest[:, 1, :], m_rest[:, 0, :], m_bf[:, 0, :], ALU.subtract).then_inc(s_ms, 1)
                    dve.wait_ge(s_mr, g + 1)
                    dve.tensor_copy(m_parts[:, 0, :], m_bf[:, 0, :])
                if stage == 2:
                    dve.wait_ge(s_ms, at + 3)
                    dve.tensor_copy(m_bf[:, 1, :], m_rest[:, 1, :]).then_inc(s_ms, 1)
                if stage == 3:
                    dve.wait_ge(s_ms, at + 4)
                    dve.tensor_copy(m_parts[:, 1, :], m_bf[:, 1, :])
                    dve.tensor_tensor(m_parts[:, 2, :], m_rest[:, 1, :], m_bf[:, 1, :], ALU.subtract).then_inc(s_mp, 1)

            def take_max(b, h, qt, before):
                if before and qt < 4:
                    split_max(b, h - 1, qt)
                    if qt == 0:
                        dve.wait_ge(s_ms, (b * HEADS + h - 1) * 4 + 2)
                dve.wait_ge(s_sc, (b * HEADS + h) * TT + (qt + 1))
                dve.tensor_reduce(neg_max[:, qt:qt + 1], pair(qt % 2), AX.X, ALU.max, negate=True).then_inc(s_mx, 1)

            def normalise(b, h):
                g = b * HEADS + h
                o = ps[:, 6, 0:TT * VC].rearrange("p (t c) -> p t c", c=VC)
                dve.wait_ge(s_ot, g + 2)
                dve.reciprocal(r_sum[:, :, :], o[:, :, HD:HD + 1]).then_inc(s_rc, 1)
                dve.wait_ge(s_rc, g + 1)
                dve.tensor_tensor(att[:, :, ds(h * HD, HD)], o[:, :, 0:HD], r_sum[:, :, :].broadcast_to([P, TT, HD]),
                                  ALU.mult).then_inc(s_nm, 1)

            def step(b, h, before):
                for qt in range(TT):
                    take_max(b, h + PRE, qt, True)
                    if qt == 4 and before:
                        normalise(b, h - 1)

            def heads(b, more):
                dve.wait_ge(s_done, (b + 1) * 16)
                step(b, 0, False)
                with dve.Fori(1, HEADS - PRE) as h:
                    step(b, h, True)
                for stage in range(4):
                    split_max(b, HEADS - 1, stage)
                if more:
                    take_x(b + 1, 0)
                    take_x(b + 1, 1)
                normalise(b, HEADS - 3)
                if more:
                    split_qk(b + 1, 0)
                    split_qk(b + 1, 1)
                    split_qk(b + 1, 2)
                normalise(b, HEADS - 2)
                if more:
                    split_qk(b + 1, 3)
                normalise(b, HEADS - 1)
                dve.wait_ge(s_nm, (b + 1) * HEADS + 1)
                dve.wait_ge(s_ea, (b + 1) * EU + EBANKS)
                dve.tensor_tensor(att[:, :, :], att[:, :, :], acc[:, :, :], ALU.add).then_inc(s_at, 1)

            def ln_sums(b):
                for t in range(TT):
                    dve.wait_ge(s_at, b + 1)
                    dve.bn_stats(stats[:, t, :], att[:, t, :]).then_inc(s_lns, 1)

            def ln_stats(b):
                dve.wait_ge(s_lns, b * (TT + 5) + TT)
                layer_norm_stats(dve, stats, ln, s_lns, lambda k: b * (TT + 5) + (TT + k)).then_inc(s_mv, 1)

            def ln_out(b):
                dve.wait_ge(s_rs, b + 1)
                for t in range(TT):
                    dve.tensor_scalar(att[:, t, :], att[:, t, :], ln[:, 0, t:t + 1], rstd[:, t:t + 1],
                                      ALU.subtract, ALU.mult).then_inc(s_y, 1)

            def experts(b, late):
                for t in range(TT):
                    dve.wait_ge(s_v, b * TT + (t + 1))
                    v = ps[:, t % 4, :]
                    dve.tensor_tensor(v_aug[:, t, :, 0:HD], v[:, 0:H].rearrange("p (h c) -> p h c", c=HD),
                                      b_vg[:, 0:H].rearrange("p (h c) -> p h c", c=HD), ALU.add)
                    dve.tensor_tensor(gate[:, t, :], v[:, H:GV], b_vg[:, H:GV], ALU.add).then_inc(s_ve, 1)
                at = b * 7
                dve.wait_ge(s_ve, (b + 1) * TT)
                dve.tensor_reduce(g_one[:, 0, :], gate[:, :, :], AX.X, ALU.max).then_inc(s_g, 1)
                dve.wait_ge(s_g, at + 1)
                dve.tensor_tensor(gate[:, :, :], gate[:, :, :], g_one[:, 0, :].unsqueeze(2).broadcast_to([P, TT, E]),
                                  ALU.subtract).then_inc(s_gl, 1)
                dve.wait_ge(s_ge, b + 1)
                dve.tensor_reduce(g_one[:, 1, :], gate[:, :, :], AX.X, ALU.add).then_inc(s_g, 1)
                dve.wait_ge(s_g, at + 2)
                dve.reciprocal(g_one[:, 2, :], g_one[:, 1, :]).then_inc(s_g, 1)
                dve.wait_ge(s_g, at + 3)
                dve.tensor_tensor(gate[:, :, :], gate[:, :, :], g_one[:, 2, :].unsqueeze(2).broadcast_to([P, TT, E]),
                                  ALU.mult).then_inc(s_g, 1)
                dve.wait_ge(s_g, at + 4)
                other = gate[:, :, :].unsqueeze(2).broadcast_to([P, TT, E, E])
                own = gate[:, :, :].unsqueeze(3).broadcast_to([P, TT, E, E])
                dve.tensor_tensor(g_cmp[:, 0, :, :, :], other, own, ALU.is_equal).then_inc(s_g, 1)
                dve.tensor_tensor(g_cmp[:, 1, :, :, :], other, own, ALU.is_gt)
                dve.wait_ge(s_g, at + 5)
                dve.tensor_tensor(g_cmp[:, 0, :, :, :], g_cmp[:, 0, :, :, :],
                                  low[:, :, :].unsqueeze(1).broadcast_to([P, TT, E, E]), ALU.mult).then_inc(s_g, 1)
                dve.wait_ge(s_g, at + 6)
                dve.tensor_tensor(g_cmp[:, 0, :, :, :], g_cmp[:, 0, :, :, :], g_cmp[:, 1, :, :, :], ALU.add).then_inc(s_g, 1)
                dve.wait_ge(s_g, at + 7)
                dve.tensor_reduce(g_cmp[:, 1, :, :, 0], g_cmp[:, 0, :, :, :], AX.X, ALU.add).then_inc(s_rk, 1)
                dve.wait_ge(s_rk, b + 1)
                dve.scalar_tensor_tensor(out=comb[:, :, :], in0=g_cmp[:, 1, :, :, 0], scalar=1.5, in1=gate[:, :, :],
                                         op0=ALU.is_lt, op1=ALU.mult).then_inc(s_cb, 1)
                for t in range(TT):
                    for e in range(E):
                        u = t * (E // 2) + e // 2
                        if e % 2 == 0:
                            dve.wait_ge(s_ex, b * EU + (u + 1))
                            if e:
                                dve.wait_ge(s_ea, b * EU + (u + EBANKS))
                            elif t == 2:
                                dve.wait_ge(s_eba, (b + 1) * 4)
                            else:
                                dve.wait_ge(s_cb, b + 1)
                        else:
                            dve.wait_ge(s_es, b * EU + (u + 1))
                        dve.scalar_tensor_tensor(out=acc[:, t, :], in0=ps[:, 4 + u % EBANKS, (e % 2) * H:(e % 2 + 1) * H],
                                                 scalar=comb[:, t, e:e + 1], in1=(acc if e else x_in)[:, t, :],
                                                 op0=ALU.mult, op1=ALU.add).then_inc(s_ea if e % 2 else s_es, 1)
                        if t >= EARLY and e % 2 == 0:
                            unit = u - EARLY * (E // 2)
                            take_max(b, unit // TT, unit % TT, unit >= TT)
                    if t == 0 and late is not None:
                        ln_sums(late)
                    if t == 1:
                        if late is not None:
                            ln_stats(late)
                        dve.wait_ge(s_eb, b + 1)
                        for i in range(4):
                            if i == 0:
                                dve.wait_ge(s_ea, b * EU + (8 + EBANKS))
                            to = (x_in if i else acc)[:, 2 * i:2 * i + 2, :].rearrange("p t h -> p (t h)")
                            dve.tensor_tensor(to, to, ps[:, i, :], ALU.add).then_inc(s_eba, 1)
                    if t == 3 and late is not None:
                        ln_out(late)

            for k in range(KH):
                take_x(0, k)
            for mt in range(2 * KH):
                split_qk(0, mt)
            experts(0, None)
            with dve.Fori(0, NB - 1) as b:
                heads(b, True)
                experts(b + 1, b)
            heads(NB - 1, False)
            ln_sums(NB - 1)
            ln_stats(NB - 1)
            ln_out(NB - 1)


def build(nc, d):
    mamba_phase(nc, d)
    attention_phase(nc, d)


def kernel(**inputs):
    import ml_dtypes
    import numpy as np
    import concourse.bacc as bacc
    from concourse.bass_utils import run_bass_kernel_spmd

    a = {k: np.asarray(v) for k, v in inputs.items()}
    x = a["L0_attn_hidden_states"]

    def per_channel(v):
        v = v.reshape((M, P) + v.shape[1:])
        return np.moveaxis(v, 0, 1)

    qkv, bq = a["L0_ffn_W_qkv"], a["L0_ffn_b_qkv"]
    row_sel = np.zeros((3, 2 * NS, 2 * NS, P), np.float32)
    for n in range(2 * NS):
        row_sel[:, n, n, :] = 1.0
    fold = np.zeros((P, VC), np.float32)
    fold[np.arange(P), np.arange(P) % VC] = 1.0
    low = np.broadcast_to(np.tril(np.ones((E, E), np.float32), -1), (P, E, E))
    arrays = {
        "x": x, "xT": x.transpose(0, 2, 1),
        "w_in": a["L0_attn_w_in"].T, "w_xp": a["L0_attn_w_xproj"].T, "w_dt": a["L0_attn_w_dt"].T,
        "w_out": a["L0_attn_w_out"].T, "w_conv": per_channel(a["L0_attn_w_conv"][:, 0, :]),
        "b_dt": per_channel(a["L0_attn_b_dt"]), "d": per_channel(a["L0_attn_D"]),
        "a_log": per_channel(a["L0_attn_A_log"]),
        "ident": np.eye(P, dtype=np.float32), "row_sel": row_sel.reshape(3 * 2 * NS, 2 * NS, P).astype(ml_dtypes.bfloat16),
        "w_qk": qkv[:, 0:2 * H], "w_vg": np.concatenate([qkv[:, 2 * H:], a["L0_ffn_W_gate"]], axis=1),
        "b_qk": bq[0:2 * H].reshape(2 * KH, P).T, "b_vg": np.concatenate([bq[2 * H:], a["L0_ffn_b_gate"]])[None, :],
        "w_e": a["L0_ffn_W_experts"].transpose(1, 0, 2).reshape(H, E * H), "b_e": a["L0_ffn_b_experts"],
        "fold": fold, "low": low,
    }
    nc = bacc.Bacc("TRN2", target_bir_lowering=False, num_devices=1)
    maps, d = {}, {}
    for name, v in arrays.items():
        v = np.ascontiguousarray(v)
        maps["in_" + name] = v
        d[name] = nc.dram_tensor("in_" + name, v.shape, mybir.dt.from_np(v.dtype), kind="ExternalInput").ap()
    d["out"] = nc.dram_tensor("out", (NB, T, H), F32, kind="ExternalOutput").ap()
    d["x1"] = nc.dram_tensor("x1_scratch", (NB, T, H), F32, kind="Internal").ap()
    d["qk"] = nc.dram_tensor("qk_scratch", (3, 2 * KH * P, T), BF16, kind="Internal").ap()
    build(nc, d)
    r = run_bass_kernel_spmd(nc, [maps], core_ids=[0])
    return r.results[0]["out"]
```

```python
from contextlib import ExitStack

import concourse.bass as bass
from concourse import mybir

F32 = mybir.dt.float32
BF16 = mybir.dt.bfloat16
F32R = mybir.dt.float32r
ALU = mybir.AluOpType
ACT = mybir.ActivationFunctionType
AX = mybir.AxisListType

P = 128
NB = 8
T = 1024
TT = T // P
H = 256
KH = H // P
DIN = 512
M = DIN // P
NS = 16
R = 64
KC = 4
PAD = KC - 1
HALF = 512
HEADS = 16
HD = H // HEADS
E = 8
QR = 6 * HD
QPART = (0, 0, 1, 1, 0, 2)
KPART = (0, 1, 0, 1, 2, 0)
QM = QR + 3
VC = 32
EPS = 1e-5


def ds(start, n):
    return bass.ds(start, n)


def layer_norm_stats(dve, stats, ln, chain, value):
    mean_e, mean_o, dev_e, dev_o = (stats[:, :, i] for i in (1, 4, 2, 5))
    dve.tensor_tensor(ln[:, 0, :], mean_e, mean_o, ALU.add).then_inc(chain, 1)
    dve.tensor_tensor(ln[:, 2, :], mean_e, mean_o, ALU.subtract).then_inc(chain, 1)
    dve.tensor_tensor(ln[:, 1, :], dev_e, dev_o, ALU.add).then_inc(chain, 1)
    dve.wait_ge(chain, value(3))
    dve.scalar_tensor_tensor(out=ln[:, 2, :], in0=ln[:, 2, :], scalar=0.25, in1=ln[:, 2, :],
                             op0=ALU.mult, op1=ALU.mult).then_inc(chain, 1)
    dve.tensor_scalar(ln[:, 0, :], ln[:, 0, :], -0.5, None, ALU.mult).then_inc(chain, 1)
    dve.wait_ge(chain, value(4))
    return dve.scalar_tensor_tensor(out=ln[:, 1, :], in0=ln[:, 1, :], scalar=1.0 / H, in1=ln[:, 2, :],
                                    op0=ALU.mult, op1=ALU.add)


def mamba_phase(nc, d):
    with ExitStack() as ctx:
        def sb(name, shape, dt=F32):
            return ctx.enter_context(nc.sbuf_tensor(name, shape, dt))

        def sem(name):
            return ctx.enter_context(nc.semaphore(name))

        ps = ctx.enter_context(nc.psum_tensor("ps1", [P, 8, HALF], F32))

        def pair(i):
            return ps[:, 2 * i:2 * i + 2, :].rearrange("p a b -> p (a b)")

        w_in = sb("w_in", [P, 2, KH, 2 * DIN], F32R)
        w_xp = sb("w_xp", [P, M, R + 2 * NS])
        w_dt = sb("w_dt", [R, DIN])
        w_out = sb("w_out", [P, M, H])
        w_conv = sb("w_conv", [P, M, KC])
        b_dt = sb("b_dt", [P, M])
        d_col = sb("d_col", [P, M])
        a_col = sb("a_col", [P, M, NS])
        ident = sb("ident1", [P, P])
        d_diag = sb("d_diag", [P, M, P])
        row_sel = sb("row_sel", [3 * 2 * NS, 2 * NS, P], BF16)
        one_col = sb("one_col1", [P, 1])
        xT = sb("xT", [P, 2, KH, T], F32R)
        x_nat = sb("x_nat", [P, TT, H])
        h_raw = sb("h_raw", [P, M, PAD + T])
        hs = sb("hs", [P, M, T])
        s_res = sb("s_res", [P, M, T])
        bc_parts = sb("bc_parts", [3 * 2 * NS, T], BF16)
        bc_mid = sb("bc_mid", [2 * NS, T], BF16)
        sp_x = sb("sp_x", [P, 2, T])
        delta = sb("delta", [P, M, T])
        u = sb("u", [P, M, T])
        dt, bc_rest = u[0:R, 0, :], u[0:2 * NS, 1, :]
        dA = sb("dA", [P, 2, T])
        raw_w = dA
        raw_x = [h_raw[:, k, PAD:PAD + T] for k in range(KH)]
        dBx = sb("dBx", [P, 2, T])
        z = sb("z", [P, 2, T])
        zC = sb("zC", [P, 2, T])
        c_rows = sb("c_rows", [P, 2, T])
        conv = (z[:, 0, :], z[:, 1, :], dBx[:, 0, :], dBx[:, 1, :])
        sp_e = (dA[:, 0, :], dA[:, 1, :], zC[:, 0, :], zC[:, 1, :])
        sp_l = (c_rows[:, 0, :], c_rows[:, 1, :], sp_x[:, 0, :], sp_x[:, 1, :])
        sp_d = (dBx[:, 0, :], dBx[:, 1, :], z[:, 0, :], z[:, 1, :])
        yg = sb("yg", [P, M, T])
        stats = sb("stats1", [P, TT, 6])
        ln = sb("ln1", [P, 3, TT])
        eps_col = sb("eps_col1", [P, 1])
        rstd = sb("rstd1", [P, TT])

        s_wi = sem("w_in_loaded")
        s_w = sem("weights_loaded1")
        s_const = sem("constants_ready1")
        s_a = sem("a_exp_done")
        s_wh = sem("w_in_high_part")
        s_ws = sem("w_in_split")
        s_xt = sem("xT_loaded")
        s_xh = sem("xT_high_part")
        s_xl = sem("xT_low_part")
        s_xn = sem("x_loaded")
        s_in = sem("in_proj_done")
        s_ev = sem("in_proj_taken")
        s_cv = sem("conv_step")
        s_cvd = sem("conv_done")
        s_cvp = sem("conv_step_pool")
        s_cvpd = sem("conv_done_pool")
        s_hs = sem("hs_done")
        s_xp = sem("x_proj_done")
        s_dt = sem("dt_taken")
        s_bcs = sem("bc_split_step")
        s_bc = sem("bc_parts_done")
        s_dtp = sem("dt_proj_done")
        s_abs = sem("abs_done")
        s_relu = sem("relu_done")
        s_exp = sem("exp_done")
        s_ln = sem("log_done")
        s_spc = sem("softplus_step")
        s_dl = sem("delta_done")
        s_spp = sem("softplus_step_pool")
        s_dlp = sem("delta_done_pool")
        s_u = sem("u_done")
        s_b = sem("b_rows_ready")
        s_c = sem("c_rows_ready")
        s_cs = sem("c_rows_taken")
        s_da = sem("dA_ready")
        s_dbx = sem("dBx_ready")
        s_z = sem("z_ready")
        s_zc = sem("zC_ready")
        s_y = sem("zC_added")
        s_yg = sem("y_gated")
        s_o = sem("out_proj_done")
        s_r = sem("residual_added")
        s_lns = sem("ln1_step")
        s_ve = sem("mean_var_done")
        s_lv = sem("log_var_done")
        s_rs = sem("rstd_done")
        s_xc = sem("x1_centred")
        s_x1 = sem("x1_done")
        s_st = sem("x1_stored")

        TERMS = tuple((k, w, x) for k in range(KH) for w, x in ((0, 0), (0, 1), (1, 0)))
        block = ctx.enter_context(nc.Block())

        UNITS = M // 2 * NS
        CONSTS = M + 4
        WEIGHTS = 16 * 9
        ORDER = (2, 3, 0, 1)
        CONV_END = ORDER[1:] + ORDER[:1]

        @block.sync
        def _(sp):
            def load_xT(b):
                for k in range(KH):
                    sp.dma_start(raw_x[k], d["xT"][ds(b, 1), k * P:(k + 1) * P, :].rearrange("o p t -> p (o t)")).then_inc(s_xt, 16)

            def load_x(b):
                sp.dma_start(x_nat[:, :, :], d["x"][ds(b, 1)].rearrange("o (t p) h -> p (o t) h", p=P)).then_inc(s_xn, 16)

            def store_x1(b):
                sp.wait_ge(s_x1, (b + 1) * TT)
                sp.dma_start(d["x1"][ds(b, 1)].rearrange("o (t p) h -> p (o t) h", p=P), x_nat[:, :, :]).then_inc(s_st, 16)

            sp.dma_start(raw_w[:, :, :], d["w_in"].rearrange("(k p) n -> p k n", p=P)).then_inc(s_wi, 16)
            load_xT(0)
            for dst, src in ((w_xp, d["w_xp"]), (w_out, d["w_out"])):
                sp.dma_start(dst[:, :, :], src.rearrange("(k p) n -> p k n", p=P)).then_inc(s_w, 16)
            sp.dma_start(w_dt[:, :], d["w_dt"]).then_inc(s_w, 16)
            for dst, src in ((w_conv, d["w_conv"]), (a_col, d["a_log"]), (row_sel, d["row_sel"])):
                sp.dma_start(dst[:, :, :], src).then_inc(s_w, 16)
            for dst, src in ((b_dt, d["b_dt"]), (d_col, d["d"]), (ident, d["ident"])):
                sp.dma_start(dst[:, :], src).then_inc(s_w, 16)
            load_x(0)
            def next_xT(b):
                sp.wait_ge(s_cvd, (b + 1) * (M - 1))
                sp.wait_ge(s_cvpd, b + 1)
                load_xT(b + 1)

            def next_x(b):
                store_x1(b)
                sp.wait_ge(s_st, (b + 1) * 16)
                load_x(b + 1)

            next_xT(0)
            with sp.Fori(0, NB - 2) as b:
                next_xT(b + 1)
                next_x(b)
            next_x(NB - 2)
            store_x1(NB - 1)
            sp.wait_ge(s_st, NB * 16)

        @block.gpsimd
        def _(pool):
            pool.sem_inc(s_zc, 4)
            pool.memset(h_raw[:, :, 0:PAD], 0.0).then_inc(s_const, 1)
            pool.memset(one_col[:, :], 1.0).then_inc(s_const, 1)
            pool.memset(eps_col[:, :], EPS).then_inc(s_const, 1)
            pool.wait_ge(s_w, WEIGHTS)
            for m in range(M):
                pool.tensor_scalar(d_diag[:, m, :], ident[:, :], d_col[:, m:m + 1], None, ALU.mult).then_inc(s_const, 1)
            pool.wait_ge(s_a, 1)
            pool.tensor_scalar(a_col[:, :, :], a_col[:, :, :], -1.0, None, ALU.mult).then_inc(s_const, 1)
            pool.wait_ge(s_const, CONSTS)

            def conv_pool(b):
                m = ORDER[0]
                at = b * (2 * KC - 3)
                pool.wait_ge(s_ev, b * (2 * M) + 1)
                for j in range(KC):
                    tap = sp_x[:, j % 2, :] if j else conv[m]
                    weight = w_conv[:, m, j:j + 1].broadcast_to([P, T])
                    mult = pool.tensor_tensor(tap, h_raw[:, m, j:j + T], weight, ALU.mult)
                    if j:
                        mult.then_inc(s_cvp, 1)
                        pool.wait_ge(s_cvp, at + (2 * j - 1))
                        pool.tensor_tensor(conv[m], conv[m], tap, ALU.add).then_inc(s_cvp if j < KC - 1 else s_cvpd, 1)
                        if j < KC - 1:
                            pool.wait_ge(s_cvp, at + 2 * j)

            def softplus_pool(b):
                m = M - 1
                ones = one_col[:, :].broadcast_to([P, T])
                pool.wait_ge(s_exp, b * M + 1)
                pool.tensor_tensor(sp_d[m], sp_e[m], ones, ALU.add).then_inc(s_spp, 1)
                pool.wait_ge(s_spp, b * 4 + 1)
                pool.tensor_tensor(sp_d[m], sp_d[m], ones, ALU.subtract).then_inc(s_spp, 1)
                pool.wait_ge(s_spp, b * 4 + 2)
                pool.tensor_tensor(sp_d[m], sp_e[m], sp_d[m], ALU.subtract).then_inc(s_spp, 1)
                pool.wait_ge(s_spp, b * 4 + 3)
                pool.wait_ge(s_ln, b * M + 1)
                pool.tensor_tensor(sp_d[m], sp_l[m], sp_d[m], ALU.add).then_inc(s_spp, 1)
                pool.wait_ge(s_spp, b * 4 + 4)
                pool.wait_ge(s_relu, b * M + (m + 1))
                pool.tensor_tensor(delta[:, m, :], delta[:, m, :], sp_d[m], ALU.add).then_inc(s_dlp, 1)

            with pool.Fori(0, NB) as b:
                conv_pool(b)
                softplus_pool(b)
                for m in range(M):
                    if m < M - 1:
                        pool.wait_ge(s_dl, b * (M - 1) + (m + 1))
                    else:
                        pool.wait_ge(s_dlp, b + 1)
                    pool.tensor_tensor(u[:, m, :], delta[:, m, :], hs[:, m, :], ALU.mult).then_inc(s_u, 1)
                for mp in range(M // 2):
                    with pool.Fori(0, NS // 2) as n2:
                        for k in range(2):
                            i = b * UNITS + n2 * 2 + (mp * NS + k)
                            for mi in range(2):
                                pool.wait_ge(s_z, i * 2 + (mi + 3))
                                pool.wait_ge(s_cs, i + 2)
                                pool.wait_ge(s_y, i * 2 + (mi + 1))
                                pool.tensor_tensor(zC[:, mi, :], z[:, mi, :], c_rows[:, k, :], ALU.mult).then_inc(s_zc, 1)

        @block.tensor
        def _(pe):
            pe.sem_inc(s_y, 2)
            pe.wait_ge(s_ws, 1)

            def sel_of(n):
                return row_sel[:, ds(n, 1), :].rearrange("p o c -> p (o c)")

            def rows(i, n):
                pe.wait_ge(s_dbx, i * 2 + 2)
                for half in range(2):
                    mm = pe.matmul(ps[:, 4 + half, :], sel_of(n), bc_parts[:, half * HALF:(half + 1) * HALF],
                                   start=True, stop=True)
                mm.then_inc(s_b, 1)
                pe.wait_ge(s_cs, i + 1)
                for half in range(2):
                    mm = pe.matmul(ps[:, 6 + half, :], sel_of(n + NS), bc_parts[:, half * HALF:(half + 1) * HALF],
                                   start=True, stop=True)
                mm.then_inc(s_c, 1)

            def add(i, mi, first=False, last=False):
                pe.wait_ge(s_zc, i * 2 + (mi + 5))
                for half in range(2):
                    mm = pe.matmul(ps[:, 2 * mi + half, :], ident[:, :], zC[:, mi, half * HALF:(half + 1) * HALF],
                                   start=first, stop=last, skip_group_check=True)
                mm.then_inc(s_y, 1)

            def d_times_hs(mp, mi, half, first):
                pe.matmul(ps[:, 2 * mi + half, :], d_diag[:, 2 * mp + mi, :],
                          hs[:, 2 * mp + mi, half * HALF:(half + 1) * HALF], start=first, stop=False, skip_group_check=True)

            def in_proj(m, to):
                for half in range(2):
                    for i, (k, w, x) in enumerate(TERMS):
                        mm = pe.matmul(ps[:, 2 * to + half, :], w_in[:, w, k, m * P:(m + 1) * P],
                                       xT[:, x, k, half * HALF:(half + 1) * HALF], start=(i == 0), stop=(i == len(TERMS) - 1))
                mm.then_inc(s_in, 1)

            def out_proj(b):
                for t in range(TT):
                    for m in range(M):
                        mm = pe.matmul(ps[:, (6 if t < 4 else 4) + t % 4 // 2, (t % 2) * H:(t % 2 + 1) * H],
                                       yg[:, m, t * P:(t + 1) * P], w_out[:, m, :], start=(m == 0), stop=(m == M - 1))
                    if t % 4 == 3:
                        mm.then_inc(s_o, 1)

            def first_in_proj(b):
                pe.wait_ge(s_xl, (b + 1) * KH)
                pe.wait_ge(s_dbx, b * (2 * UNITS) + 2)
                in_proj(ORDER[0], ORDER[0])

            def batch(b, first, last):
                pe.wait_ge(s_cs, b * UNITS + 1)
                for j, m in enumerate(ORDER):
                    if j == 2 and not first:
                        pe.wait_ge(s_yg, b * M)
                    if j:
                        in_proj(m, m)
                pe.wait_ge(s_ev, b * (2 * M) + 3)
                in_proj(M, 0)
                pe.wait_ge(s_ev, b * (2 * M) + 4)
                in_proj(M + 1, 1)
                if first:
                    pe.wait_ge(s_w, WEIGHTS)
                    pe.wait_ge(s_const, CONSTS)
                for j, m in enumerate(CONV_END):
                    pe.wait_ge(s_hs, b * M + (j + 1))
                    for half in range(2):
                        mm = pe.matmul(ps[0:R + 2 * NS, 4 + half, :], w_xp[:, m, :], hs[:, m, half * HALF:(half + 1) * HALF],
                                       start=(j == 0), stop=(j == M - 1))
                mm.then_inc(s_xp, 1)
                pe.wait_ge(s_dt, b + 1)
                for m in range(M):
                    if m in (1, 2):
                        pe.wait_ge(s_ev, b * (2 * M) + (M + m))
                    if m == M - 1:
                        pe.wait_ge(s_bcs, b * 3 + 2)
                    for half in range(2):
                        mm = pe.matmul(ps[:, 2 * ((m + 3) % M) + half, :], w_dt[:, m * P:(m + 1) * P],
                                       dt[:, half * HALF:(half + 1) * HALF], start=True, stop=True)
                    mm.then_inc(s_dtp, 1)
                pe.wait_ge(s_abs, b * M + 2)
                pe.wait_ge(s_relu, b * M + 2)
                in_proj(M + 2, 0)
                pe.wait_ge(s_abs, b * M + 3)
                pe.wait_ge(s_relu, b * M + 3)
                in_proj(M + 3, 1)
                pe.wait_ge(s_abs, (b + 1) * M)
                pe.wait_ge(s_relu, (b + 1) * M)
                if not first:
                    out_proj(b - 1)
                pe.wait_ge(s_bc, b + 1)
                for mp in range(M // 2):
                    i0 = b * UNITS + mp * NS
                    if not mp:
                        for mi in range(2):
                            pe.wait_ge(s_ev, b * (2 * M) + (M + 3 + mi))
                            for half in range(2):
                                d_times_hs(mp, mi, half, True)
                            if mi == 0:
                                if not first:
                                    pe.wait_ge(s_r, b * 2)
                                rows(i0, 0)
                                rows(i0 + 1, 1)
                    else:
                        for n in range(6):
                            for mi in range(2):
                                if n == 0:
                                    pe.wait_ge(s_yg, b * M + (mi + 1))
                                add(i0 + n, mi, first=(n == 0))
                                if mi == 0:
                                    rows(i0 + n + 2, n + 2)
                            if 1 <= n <= 4:
                                d_times_hs(mp, (n - 1) // 2, (n - 1) % 2, False)
                    with pe.Fori(3 if mp else 0, NS // 2 - 1) as n2:
                        for k in range(2):
                            n = n2 * 2 + k
                            add(i0 + n, 0)
                            rows(i0 + n + 2, n + 2)
                            add(i0 + n, 1)
                    for n in (NS - 2, NS - 1):
                        if mp and n == NS - 1 and not last:
                            first_in_proj(b + 1)
                        add(i0 + n, 0, last=(n == NS - 1))
                        if not mp:
                            rows(i0 + n + 2, n + 2 - NS)
                        add(i0 + n, 1, last=(n == NS - 1))

            first_in_proj(0)
            batch(0, True, False)
            with pe.Fori(1, NB - 1) as b:
                batch(b, False, False)
            batch(NB - 1, False, True)
            pe.wait_ge(s_yg, NB * M)
            pe.wait_ge(s_dbx, NB * 2 * UNITS + 2)
            pe.wait_ge(s_cs, NB * UNITS + 1)
            out_proj(NB - 1)

        @block.scalar
        def _(act):
            act.sem_inc(s_cs, 1)

            def high_x(b):
                for k in range(KH):
                    act.wait_ge(s_xt, (b + 1) * (16 * KH))
                    act.activation(xT[:, 0, k, :], raw_x[k], ACT.Copy).then_inc(s_xh, 1)

            high_x(0)
            act.wait_ge(s_w, WEIGHTS)
            act.activation(a_col[:, :, :], a_col[:, :, :], ACT.Exp).then_inc(s_a, 1)
            act.wait_ge(s_const, CONSTS)

            def gate_silu(b, m):
                act.wait_ge(s_in, b * (2 * M) + (M + m + 1))
                act.activation(s_res[:, m, :], pair(m % 2), ACT.Silu).then_inc(s_ev, 1)

            def conv_silu(b, j):
                act.wait_ge(*((s_cvd, b * (M - 1) + (j + 1)) if j < M - 1 else (s_cvpd, b + 1)))
                act.activation(hs[:, CONV_END[j], :], conv[CONV_END[j]], ACT.Silu).then_inc(s_hs, 1)

            def inv_std(b):
                act.wait_ge(s_ve, b + 1)
                act.activation(rstd[:, :], ln[:, 1, :], ACT.Ln, bias=eps_col[:, :]).then_inc(s_lv, 1)
                act.wait_ge(s_lv, b + 1)
                act.activation(rstd[:, :], rstd[:, :], ACT.Exp, scale=-0.5).then_inc(s_rs, 1)

            def ln_out(b, first, last):
                act.wait_ge(s_rs, b + 1)
                for t in range(first, last):
                    act.activation(x_nat[:, t, :], x_nat[:, t, :], ACT.Identity, bias=ln[:, 0, t:t + 1]).then_inc(s_xc, 1)
                for t in range(first, last):
                    act.wait_ge(s_xc, b * TT + (t + 1))
                    act.activation(x_nat[:, t, :], x_nat[:, t, :], ACT.Copy, scale=rstd[:, t:t + 1]).then_inc(s_x1, 1)

            def decays(b, mp, n2):
                for k in range(2):
                    i = b * UNITS + n2 * 2 + (mp * NS + k)
                    for mi in range(2):
                        m = 2 * mp + mi
                        act.wait_ge(s_z, i * 2 + (mi + 1))
                        act.activation(dA[:, mi, :], delta[:, m, :], ACT.Exp,
                                       scale=a_col[:, m, ds(n2 * 2 + k, 1)]).then_inc(s_da, 1)
                        if mi == 0:
                            act.wait_ge(s_c, i + 1)
                            act.wait_ge(s_zc, i * 2 + 2)
                            act.activation(c_rows[:, k, :], pair(3), ACT.Copy).then_inc(s_cs, 1)

            def batch(b, first, last):
                for j, m in enumerate(ORDER):
                    act.wait_ge(s_in, b * (2 * M) + (j + 1))
                    act.activation(h_raw[:, m, PAD:PAD + T], pair(m), ACT.Copy).then_inc(s_ev, 1)
                conv_silu(b, 0)
                conv_silu(b, 1)
                gate_silu(b, 0)
                conv_silu(b, 2)
                gate_silu(b, 1)
                conv_silu(b, 3)
                act.wait_ge(s_xp, b + 1)
                act.activation(dt, pair(2)[0:R, :], ACT.Copy).then_inc(s_dt, 1)
                for m in range(M):
                    act.wait_ge(s_dtp, b * M + (m + 1))
                    pr = pair((m + 3) % M)
                    act.activation(sp_e[m], pr, ACT.Abs, bias=b_dt[:, m:m + 1]).then_inc(s_abs, 1)
                for m in (M - 1, 0, 1, 2):
                    act.wait_ge(s_abs, b * M + (m + 1))
                    act.activation(sp_e[m], sp_e[m], ACT.Exp, scale=-1.0).then_inc(s_exp, 1)
                for j, m in enumerate((M - 1, 0, 1, 2)):
                    act.wait_ge(s_exp, b * M + (j + 1))
                    act.activation(sp_l[m], sp_e[m], ACT.Ln, bias=one_col[:, :]).then_inc(s_ln, 1)
                gate_silu(b, 2)
                gate_silu(b, 3)
                if not last:
                    act.wait_ge(s_in, (b + 1) * (2 * M))
                    high_x(b + 1)
                act.wait_ge(s_dl, b * (M - 1) + 2)
                with act.Fori(0, NS // 2) as n2:
                    decays(b, 0, n2)
                if not first:
                    inv_std(b - 1)
                act.wait_ge(s_dl, (b + 1) * (M - 1))
                act.wait_ge(s_dlp, b + 1)
                for n2 in range(4):
                    decays(b, 1, n2)
                    if not first:
                        ln_out(b - 1, 2 * n2, 2 * n2 + 2)
                with act.Fori(4, NS // 2) as n2:
                    decays(b, 1, n2)

            batch(0, True, False)
            with act.Fori(1, NB - 1) as b:
                batch(b, False, False)
            batch(NB - 1, False, True)
            inv_std(NB - 1)
            ln_out(NB - 1, 0, TT)

        @block.vector
        def _(dve):
            dve.sem_inc(s_z, 2)
            dve.sem_inc(s_dbx, 2)

            def low_x(b):
                for k in range(KH):
                    dve.wait_ge(s_xh, b * KH + (k + 1))
                    dve.tensor_tensor(xT[:, 1, k, :], raw_x[k], xT[:, 0, k, :], ALU.subtract).then_inc(s_xl, 1)

            dve.wait_ge(s_wi, 16)
            dve.tensor_copy(w_in[:, 0, :, :], raw_w[:, :, :]).then_inc(s_wh, 1)
            dve.wait_ge(s_wh, 1)
            dve.tensor_tensor(w_in[:, 1, :, :], raw_w[:, :, :], w_in[:, 0, :, :], ALU.subtract).then_inc(s_ws, 1)
            low_x(0)
            dve.wait_ge(s_w, WEIGHTS)
            dve.wait_ge(s_const, CONSTS)

            def conv_dve(b):
                for j, m in enumerate(ORDER[1:]):
                    dve.wait_ge(s_ev, b * (2 * M) + (j + 2))
                    dve.tensor_scalar(conv[m], h_raw[:, m, 0:T], w_conv[:, m, 0:1], None, ALU.mult).then_inc(s_cv, 1)
                    for tap in range(1, KC):
                        dve.wait_ge(s_cv, b * ((M - 1) * (KC - 1)) + (j * (KC - 1) + tap))
                        dve.scalar_tensor_tensor(out=conv[m], in0=h_raw[:, m, tap:tap + T], scalar=w_conv[:, m, tap:tap + 1],
                                                 in1=conv[m], op0=ALU.mult, op1=ALU.add)\
                           .then_inc(s_cv if tap < KC - 1 else s_cvd, 1)

            def split_bc(b):
                dve.wait_ge(s_xp, b + 1)
                bc = pair(2)[R:R + 2 * NS, :]
                q = 2 * NS
                dve.tensor_copy(bc_parts[0:q, :], bc).then_inc(s_bcs, 1)
                dve.wait_ge(s_bcs, b * 3 + 1)
                dve.tensor_tensor(bc_rest, bc, bc_parts[0:q, :], ALU.subtract).then_inc(s_bcs, 1)
                dve.wait_ge(s_bcs, b * 3 + 2)
                dve.tensor_copy(bc_mid[:, :], bc_rest).then_inc(s_bcs, 1)
                dve.wait_ge(s_bcs, b * 3 + 3)
                dve.tensor_copy(bc_parts[q:2 * q, :], bc_mid[:, :])
                dve.tensor_tensor(bc_parts[2 * q:3 * q, :], bc_rest, bc_mid[:, :], ALU.subtract).then_inc(s_bc, 1)

            def softplus_end(b):
                for m in range(M):
                    dve.wait_ge(s_abs, b * M + (m + 1))
                    dve.tensor_scalar(delta[:, m, :], pair((m + 3) % M), b_dt[:, m:m + 1], 0.0, ALU.add, ALU.max).then_inc(s_relu, 1)
                tiles = M - 1
                st = b * (3 * tiles)
                for m in range(tiles):
                    dve.wait_ge(s_exp, b * M + (m + 2))
                    dve.tensor_scalar(sp_d[m], sp_e[m], 1.0, -1.0, ALU.add, ALU.add).then_inc(s_spc, 1)
                for m in range(tiles):
                    dve.wait_ge(s_spc, st + (m + 1))
                    dve.tensor_tensor(sp_d[m], sp_e[m], sp_d[m], ALU.subtract).then_inc(s_spc, 1)
                for m in range(tiles):
                    dve.wait_ge(s_spc, st + (tiles + m + 1))
                    dve.wait_ge(s_ln, b * M + (m + 2))
                    dve.tensor_tensor(sp_d[m], sp_l[m], sp_d[m], ALU.add).then_inc(s_spc, 1)
                    dve.wait_ge(s_spc, st + (2 * tiles + m + 1))
                    dve.wait_ge(s_relu, b * M + (m + 1))
                    dve.tensor_tensor(delta[:, m, :], delta[:, m, :], sp_d[m], ALU.add).then_inc(s_dl, 1)

            def residual(b, i):
                dve.wait_ge(s_xn, (b + 1) * 16)
                dve.wait_ge(s_o, b * 2 + (i + 1))
                to = x_nat[:, 4 * i:4 * i + 4, :].rearrange("p t h -> p (t h)")
                dve.tensor_tensor(to, to, pair(3 - i), ALU.add).then_inc(s_r, 1)

            def ln_sums(b, i):
                for t in range(4 * i, 4 * i + 4):
                    dve.wait_ge(s_r, b * 2 + (i + 1))
                    dve.bn_stats(stats[:, t, :], x_nat[:, t, :]).then_inc(s_lns, 1)

            def ln_stats(b):
                dve.wait_ge(s_lns, b * (TT + 5) + TT)
                layer_norm_stats(dve, stats, ln, s_lns, lambda k: b * (TT + 5) + (TT + k)).then_inc(s_ve, 1)

            def scan(b, mp, n):
                i = b * UNITS + n + mp * NS
                dve.wait_ge(s_u, b * M + (2 * mp + 2))
                dve.wait_ge(s_b, i + 1)
                for mi in range(2):
                    dve.wait_ge(s_z, i * 2 + (mi + 1))
                    dve.tensor_tensor(dBx[:, mi, :], u[:, 2 * mp + mi, :], pair(2), ALU.mult).then_inc(s_dbx, 1)
                for mi in range(2):
                    dve.wait_ge(s_dbx, i * 2 + (mi + 3))
                    dve.wait_ge(s_da, i * 2 + (mi + 1))
                    dve.wait_ge(s_zc, i * 2 + (mi + 3))
                    dve.tensor_tensor_scan(z[:, mi, :], dA[:, mi, :], dBx[:, mi, :], 0.0,
                                           ALU.mult, ALU.add).then_inc(s_z, 1)

            def gate(b, mp):
                dve.wait_ge(s_y, b * (M * NS) + ((mp + 1) * 2 * NS + 2))
                for mi in range(2):
                    dve.tensor_tensor(yg[:, 2 * mp + mi, :], s_res[:, 2 * mp + mi, :], pair(mi), ALU.mult).then_inc(s_yg, 1)

            def batch(b, first, last):
                conv_dve(b)
                split_bc(b)
                softplus_end(b)
                if not first:
                    residual(b - 1, 0)
                if not last:
                    dve.wait_ge(s_in, (b + 1) * (2 * M))
                    low_x(b + 1)
                if not first:
                    residual(b - 1, 1)
                    ln_sums(b - 1, 0)
                scan(b, 0, 0)
                if not first:
                    ln_sums(b - 1, 1)
                    ln_stats(b - 1)
                scan(b, 0, 1)
                with dve.Fori(1, NS // 2) as n2:
                    for k in range(2):
                        scan(b, 0, n2 * 2 + k)
                scan(b, 1, 0)
                gate(b, 0)
                scan(b, 1, 1)
                with dve.Fori(1, NS // 2) as n2:
                    for k in range(2):
                        scan(b, 1, n2 * 2 + k)
                gate(b, 1)

            batch(0, True, False)
            with dve.Fori(1, NB - 1) as b:
                batch(b, False, False)
            batch(NB - 1, False, True)
            for i in range(2):
                residual(NB - 1, i)
                ln_sums(NB - 1, i)
            ln_stats(NB - 1)

def attention_phase(nc, d):
    with ExitStack() as ctx:
        def sb(name, shape, dt=F32):
            return ctx.enter_context(nc.sbuf_tensor(name, shape, dt))

        def sem(name):
            return ctx.enter_context(nc.semaphore(name))

        ps = ctx.enter_context(nc.psum_tensor("ps2", [P, 8, HALF], F32))

        def pair(i):
            return ps[:, 2 * i:2 * i + 2, :].rearrange("p a b -> p (a b)")

        GV = H + E
        QUARTERS = P // VC
        w_qk = sb("w_qk", [P, 2, KH, 2 * H], F32R)
        w_vg = sb("w_vg", [P, 2, KH, GV], F32R)
        w_e = sb("w_e", [P, 2, KH, E * H], F32R)
        b_e = sb("b_e", [E, H])
        b_qk = sb("b_qk", [P, 2 * KH])
        b_vg = sb("b_vg", [P, GV])
        ident = sb("ident2", [P, P])
        low = sb("low", [P, E, E])
        eps_col = sb("eps_col2", [P, 1])
        x_in = sb("x_in", [P, TT, H])
        acc = sb("acc", [P, TT, H])
        x1T = sb("x1T", [P, 2, KH, T], F32R)
        qk_parts = sb("qk_parts", [P, 3, 2, T], BF16)
        q_st = sb("q_st", [QM, HEADS, T], BF16)
        k_st = sb("k_st", [QM, HEADS, T], BF16)
        v_all = sb("v_all", [P, TT, H])
        v_h = sb("v_h", [P, TT, VC])
        gate = sb("gate", [P, TT, E])
        g_one = sb("g_one", [P, 3, TT])
        comb = sb("comb", [P, TT, E])
        neg_max = sb("neg_max", [P, TT])
        m_rest = sb("m_rest", [P, 2, TT])
        m_bf = sb("m_bf", [P, 2, TT], BF16)
        m_parts = sb("m_parts", [P, 3, TT])
        m_rows = sb("m_rows", [3 * TT, P], BF16)
        probs = sb("probs", [P, TT, T])
        g_cmp = probs[:, 0, :].rearrange("p (s t e f) -> p s t e f", s=2, t=TT, e=E)
        combT = probs[0:E, 1, :]
        scaled = probs[:, 2, :].rearrange("p (s e n) -> p s e n", s=2, e=2)
        raw_e = probs[:, 0:4, :].rearrange("p t n -> p (t n)").rearrange("p (k n) -> p k n", k=KH)
        raw_qk = probs[:, 4, :].rearrange("p (k n) -> p k n", k=KH)
        raw_vg = probs[:, 5, 0:KH * GV].rearrange("p (k n) -> p k n", k=KH)
        o_sb = sb("o_sb", [P, T // QUARTERS])
        r_sum = sb("r_sum", [P, 2, QUARTERS, 1])
        att = sb("att", [P, TT, H])
        stats = sb("stats2", [P, TT, 6])
        ln = sb("ln2", [P, 3, TT])
        rstd = sb("rstd2", [P, TT])

        s_wq = sem("qk_weights_loaded")
        s_w = sem("weights_loaded2")
        s_const = sem("constants_ready2")
        s_wh = sem("weights_high_part")
        s_wa = sem("weights_high_part_scalar")
        s_ws = sem("weights_split")
        s_we = sem("expert_weights_split")
        s_x = sem("x1_loaded")
        s_xh = sem("x1T_high_part")
        s_xt = sem("x1_transposed")
        s_xte = sem("x1T_ready")
        s_qk = sem("qk_proj_done")
        s_sp = sem("qk_split_step")
        s_parts = sem("qk_parts_done")
        s_qst = (sem("qk_parts_stored_even"), sem("qk_parts_stored_odd"))
        s_stk = sem("stacks_loaded")
        s_v = sem("v_gate_proj_done")
        s_ve = sem("v_gate_taken")
        s_g = sem("gate_step")
        s_gl = sem("gate_logits_shifted")
        s_ge = sem("gate_exp_done")
        s_rk = sem("gate_ranked")
        s_cb = sem("combine_done")
        s_cbt = sem("combine_transposed")
        s_cbe = sem("combT_ready")
        s_ex = sem("expert_pair_done")
        s_es = sem("expert_first_added")
        s_ea = sem("expert_pair_added")
        s_ec = sem("expert_pair_scaled")
        s_pa = sem("scaled_expert_added")
        s_fa = sem("expert_sums_joined")
        s_eb = sem("expert_bias_done")
        s_eba = sem("expert_bias_added")
        s_sc = sem("scores_ready")
        s_mx = sem("max_done")
        s_ms = sem("max_split_step")
        s_mp = sem("max_parts_done")
        s_mt = sem("max_transposed")
        s_mr = sem("max_rows_ready")
        s_md = sem("max_rows_stacked")
        s_st = sem("scoresT_ready")
        s_p = sem("probs_ready")
        s_vh = sem("v_head_ready")
        s_pv = sem("pv_tile_done")
        s_o = sem("o_taken")
        s_ot = sem("o_transposed")
        s_rc = sem("row_sum_inverted")
        s_nm = sem("head_normalised")
        s_at = sem("attention_added")
        s_lns = sem("ln2_step")
        s_mv = sem("mean_var_done2")
        s_lv = sem("log_var_done2")
        s_rs = sem("rstd_done2")
        s_yc = sem("out_tile_centred")
        s_y = sem("out_tile_done")
        s_done = sem("out_stored")

        WEIGHTS = 16 * 5
        CONSTS = 4
        PRE = 2
        EU = TT * E // 2
        EARLY = tuple(u for u in range(13, EU) if u % 2 or u in (16, 20, 22, 24, 26, 28))
        EBANK = tuple((u + 4) % 8 if u < 8 else 4 + u % 3 for u in range(EU))
        EPREV = tuple(max((v for v in range(u) if EBANK[v] == EBANK[u]), default=None) for u in range(EU))
        TERMS = tuple((k, w, x) for k in range(KH) for w, x in ((0, 0), (0, 1), (1, 0)))
        block = ctx.enter_context(nc.Block())

        @block.sync
        def _(sp):
            def load_x(b):
                sp.dma_start(x_in[:, :, :], d["x1"][ds(b, 1)].rearrange("o (t p) h -> p (o t) h", p=P)).then_inc(s_x, 16)

            load_x(0)
            sp.dma_start(ident[:, :], d["ident"]).then_inc(s_wq, 16)
            sp.dma_start(raw_qk, d["w_qk"].rearrange("(k p) n -> p k n", p=P)).then_inc(s_wq, 16)
            sp.dma_start(b_qk[:, :], d["b_qk"]).then_inc(s_wq, 16)
            for dst, src in ((raw_vg, d["w_vg"]), (raw_e, d["w_e"])):
                sp.dma_start(dst, src.rearrange("(k p) n -> p k n", p=P)).then_inc(s_w, 16)
            for dst, src in ((b_e, d["b_e"]), (b_vg, d["b_vg"].broadcast_to([P, GV]))):
                sp.dma_start(dst[:, :], src).then_inc(s_w, 16)
            sp.dma_start(low[:, :, :], d["low"]).then_inc(s_w, 16)
            sp.sem_inc(s_done, 16)
            sp.sem_inc(s_md, 16)
            sp.sem_inc(s_qst[0], 16)
            sp.sem_inc(s_qst[1], 16)

            def store_parts(b):
                for mt in range(2 * KH):
                    sp.wait_ge(s_parts, b * (2 * KH) + (mt + 1))
                    sp.dma_start(d["qk"][:, mt * P:(mt + 1) * P, :].rearrange("c p t -> p c t"),
                                 qk_parts[:, :, mt % 2, :]).then_inc(s_qst[mt % 2], 16)

            def load_stacks(b):
                sp.wait_ge(s_qst[0], (b + 1) * (16 * KH) + 16)
                sp.wait_ge(s_qst[1], (b + 1) * (16 * KH) + 16)
                for j in range(6):
                    for stack, part, first in ((q_st, QPART[j], 0), (k_st, KPART[j], H)):
                        sp.dma_start(stack[j * HD:(j + 1) * HD, :, :],
                                     d["qk"][part, first:first + H, :].rearrange("(h r) t -> r h t", r=HD)).then_inc(s_stk, 16)

            def max_rows(b, h):
                sp.wait_ge(s_mr, b * HEADS + h + 2)
                for part in range(3):
                    sp.dma_start(q_st[QR + part:QR + part + 1, ds(h, 1), :].rearrange("p o (c q) -> p (o c) q", q=P),
                                 m_rows[part * TT:(part + 1) * TT, :]).then_inc(s_md, 16)

            def store_out(b):
                sp.wait_ge(s_y, (b + 1) * TT)
                sp.dma_start(d["out"][ds(b, 1)].rearrange("o (t p) h -> p (o t) h", p=P), att[:, :, :]).then_inc(s_done, 16)

            store_parts(0)
            load_stacks(0)
            with sp.Fori(0, NB - 1) as b:
                max_rows(b, 0)
                sp.wait_ge(s_fa, (b + 1) * TT)
                load_x(b + 1)
                with sp.Fori(1, HEADS) as h:
                    max_rows(b, h)
                store_parts(b + 1)
                sp.wait_ge(s_p, (b + 1) * (HEADS * 2 * TT) + 2)
                load_stacks(b + 1)
                store_out(b)
            with sp.Fori(0, HEADS) as h:
                max_rows(NB - 1, h)
            store_out(NB - 1)
            sp.wait_ge(s_done, (NB + 1) * 16)

        @block.gpsimd
        def _(pool):
            pool.sem_inc(s_pv, TT)
            pool.sem_inc(s_pa, 4)
            pool.memset(k_st[QR:QM, :, :], 1.0).then_inc(s_const, 1)
            pool.wait_ge(s_const, 1)
            pool.memset(v_h[:, :, HD:VC], 0.0).then_inc(s_const, 1)
            pool.wait_ge(s_const, 2)
            pool.memset(v_h[:, :, HD:HD + 1], 1.0).then_inc(s_const, 1)
            pool.memset(eps_col[:, :], EPS).then_inc(s_const, 1)
            pool.wait_ge(s_const, CONSTS)
            pool.wait_ge(s_wa, 2)
            pool.tensor_tensor(w_e[:, 1, :, :], raw_e, w_e[:, 0, :, :], ALU.subtract).then_inc(s_we, 1)
            with pool.Fori(0, NB) as b:
                for i in range(EU // 2):
                    to = x_in[:, i // 2, :]
                    done = b * EU + 2 * i + 4
                    pool.wait_ge(s_ec, b * (EU // 2) + (i + 1))
                    if i == 6:
                        pool.wait_ge(s_eba, b * 5 + 3)
                    for e in range(2):
                        pool.wait_ge(s_pa, done + e)
                        pool.tensor_tensor(to, to, scaled[:, i % 2, e, :], ALU.add).then_inc(s_pa, 1)
                with pool.Fori(0, HEADS) as h:
                    pool.wait_ge(s_ve, (b + 1) * TT)
                    for first, last in ((0, 5), (5, TT)):
                        pool.wait_ge(s_pv, (b * HEADS + h) * TT + last)
                        pool.tensor_copy(v_h[:, first:last, 0:HD], v_all[:, first:last, ds(h * HD, HD)]).then_inc(s_vh, 1)

        @block.tensor
        def _(pe):
            pe.wait_ge(s_wq, 16 * 3)

            def head(stack, rows, h, first, n):
                return stack[0:rows, ds(h, 1), first:first + n].rearrange("p o c -> p (o c)")

            def scores(b, h, qt, half):
                g = b * HEADS + h
                if half == 0:
                    pe.wait_ge(s_mx, g * TT + (qt + 1))
                mm = pe.matmul(ps[:, 2 * (qt % 2) + half, :], head(q_st, QR, h, qt * P, P),
                               head(k_st, QR, h, half * HALF, HALF), start=True, stop=True)
                if half == 1:
                    mm.then_inc(s_sc, 1)

            def turn_max(b, h, normalised):
                pe.wait_ge(s_nm, normalised + 1)
                pe.wait_ge(s_mp, b * HEADS + h + 1)
                pe.transpose(ps[0:3 * TT, 7, 0:P], m_parts[:, :, :].rearrange("p c t -> p (c t)"), ident[:, :]).then_inc(s_mt, 1)

            def scores_t(b, h, kt, half):
                g = b * HEADS + h
                if kt == 0 and half == 0:
                    pe.wait_ge(s_md, g * 48 + 64)
                pe.wait_ge(s_p, g * (2 * TT) + (2 * kt + half + 1))
                pe.matmul(ps[:, 4 + half, :], head(k_st, QM, h, kt * P, P),
                          head(q_st, QM, h, half * HALF, HALF), start=True, stop=True).then_inc(s_st, 1)

            def weigh_v(b, h, kt):
                g = b * HEADS + h
                pe.wait_ge(s_p, g * (2 * TT) + (2 * kt + 4))
                if kt in (0, 5):
                    pe.wait_ge(s_vh, g * 2 + (1 + kt // 5))
                if kt == 0:
                    pe.wait_ge(s_o, g + 1)
                n = T // QUARTERS
                for j in range(QUARTERS):
                    mm = pe.matmul(ps[VC * j:VC * (j + 1), 6, 0:n], v_h[:, kt, :], probs[:, kt, j * n:(j + 1) * n],
                                   start=(kt == 0), stop=(kt == TT - 1), skip_group_check=True)
                mm.then_inc(s_pv, 1)

            def turn_o(b, h, turned=False):
                g = b * HEADS + h
                if turned:
                    pe.wait_ge(s_mr, g + 4)
                pe.wait_ge(s_o, g + 2)
                pe.wait_ge(s_nm, g + 1)
                for i in range(2):
                    mm = pe.transpose(ps[:, 7, i * P:(i + 1) * P], o_sb[:, i * P:(i + 1) * P], ident[:, :])
                mm.then_inc(s_ot, 1)

            def turn_x(b, k):
                pe.wait_ge(s_x, (b + 1) * 16)
                pe.wait_ge(s_mx, b * (HEADS * TT) + 2)
                for t in range(TT):
                    mm = pe.transpose(ps[:, 2 * k + t // 4, (t % 4) * P:(t % 4 + 1) * P],
                                      x_in[:, t, k * P:(k + 1) * P], ident[:, :])
                mm.then_inc(s_xt, 1)

            def qk_proj(b, mt, half):
                if mt == 0:
                    pe.wait_ge(s_xte, (b + 1) * KH)
                if mt >= 2:
                    pe.wait_ge(s_parts, b * (2 * KH) + (mt - 1))
                for i, (k, w, x) in enumerate(TERMS):
                    mm = pe.matmul(ps[:, 2 * (mt % 2) + half, :], w_qk[:, w, k, mt * P:(mt + 1) * P],
                                   x1T[:, x, k, half * HALF:(half + 1) * HALF], start=(i == 0), stop=(i == len(TERMS) - 1))
                if half == 1:
                    mm.then_inc(s_qk, 1)

            def v_proj(b, t):
                if t < 4:
                    pe.wait_ge(s_parts, b * (2 * KH) + (3 + t // 2))
                else:
                    pe.wait_ge(s_ve, b * TT + (t - 3))
                for i, (k, w, x) in enumerate(TERMS):
                    mm = pe.matmul(ps[:, t % 4, 0:GV], x1T[:, x, k, t * P:(t + 1) * P], w_vg[:, w, k, :],
                                   start=(i == 0), stop=(i == len(TERMS) - 1))
                mm.then_inc(s_v, 1)

            def step(b, h, before, ahead, front):
                turned = ahead or h == HEADS - PRE
                for kt in range(TT):
                    for half in range(2):
                        scores_t(b, h, kt, half)
                        if ahead:
                            scores(b, h + PRE, kt, half)
                    if before and kt < 2:
                        weigh_v(b, h - 1, 5 + kt)
                    if before and kt == 1:
                        weigh_v(b, h - 1, TT - 1)
                    if kt >= 3:
                        weigh_v(b, h, kt - 3)
                    if turned and kt == 3:
                        turn_max(b, h + 1, b * HEADS + h - 1 if before else b * HEADS)
                    if before and kt == 6:
                        turn_o(b, h - 1, turned)
                    for work, args in front.get(kt, ()):
                        work(b + 1, *args)

            def heads(b, more):
                used(b, EU - 2)
                used(b, EU - 1)
                step(b, 0, False, True, {})
                with pe.Fori(1, HEADS - PRE) as h:
                    step(b, h, True, True, {})
                step(b, HEADS - 2, True, False, {} if not more else
                     {0: [(turn_x, (0,))], 1: [(turn_x, (1,))], 3: [(qk_proj, (0, 0))], 4: [(qk_proj, (0, 1))],
                      5: [(qk_proj, (1, 0))], 6: [(qk_proj, (1, 1))]})
                step(b, HEADS - 1, True, False, {} if not more else
                     {0: [(qk_proj, (2, 0))], 1: [(qk_proj, (2, 1))], 2: [(qk_proj, (3, 0))], 3: [(qk_proj, (3, 1))]})
                for kt in range(5, TT):
                    weigh_v(b, HEADS - 1, kt)
                if more:
                    for t in range(4):
                        v_proj(b + 1, t)
                turn_o(b, HEADS - 1)

            def used(b, u):
                pe.wait_ge(s_ec if u % 2 else s_ea, b * (EU // 2) + (u // 2 + 1))

            def experts(b):
                for t in range(4, TT):
                    v_proj(b, t)
                for t in range(TT):
                    for e2 in range(E // 2):
                        u = t * (E // 2) + e2
                        if EPREV[u] is not None:
                            used(b, EPREV[u])
                        if u == 3:
                            pe.wait_ge(s_nm, b * HEADS + 1)
                        if u == 4:
                            pe.wait_ge(s_ve, (b + 1) * TT)
                        for i, (k, w, x) in enumerate(TERMS):
                            mm = pe.matmul(ps[:, EBANK[u], :], x1T[:, x, k, t * P:(t + 1) * P],
                                           w_e[:, w, k, e2 * 2 * H:(e2 + 1) * 2 * H], start=(i == 0), stop=(i == len(TERMS) - 1))
                        mm.then_inc(s_ex, 1)
                        if u in EARLY:
                            unit = EARLY.index(u)
                            if unit == 0:
                                pe.wait_ge(s_stk, (b + 1) * (12 * 16))
                                pe.wait_ge(s_eba, (b + 1) * 5)
                            for half in range(2):
                                scores(b, unit // TT, unit % TT, half)
                            if unit == TT + 4:
                                turn_max(b, 0, b * HEADS)
                    if t == 1:
                        pe.wait_ge(s_cb, b + 1)
                        used(b, 4)
                        used(b, 5)
                        for q in range(TT):
                            mm = pe.transpose(ps[0:E, q // 4, (q % 4) * P:(q % 4 + 1) * P], comb[:, q, :], ident[:, :])
                        mm.then_inc(s_cbt, 1)
                    if t == 2:
                        pe.wait_ge(s_cbe, b + 1)
                        used(b, 6)
                        used(b, 7)
                        for q in range(TT):
                            mm = pe.matmul(ps[:, q // 2, (q % 2) * H:(q % 2 + 1) * H], combT[:, q * P:(q + 1) * P],
                                           b_e[:, :], start=True, stop=True)
                        mm.then_inc(s_eb, 1)

            for k in range(KH):
                turn_x(0, k)
            pe.wait_ge(s_ws, 1)
            for mt in range(2 * KH):
                for half in range(2):
                    qk_proj(0, mt, half)
            pe.wait_ge(s_ws, 2)
            pe.wait_ge(s_w, WEIGHTS)
            for t in range(4):
                v_proj(0, t)
            pe.wait_ge(s_const, CONSTS)
            pe.wait_ge(s_we, 1)
            experts(0)
            with pe.Fori(0, NB - 1) as b:
                heads(b, True)
                experts(b + 1)
            heads(NB - 1, False)

        @block.scalar
        def _(act):
            act.sem_inc(s_p, 2)
            act.sem_inc(s_mr, 1)
            act.sem_inc(s_o, 1)
            act.wait_ge(s_w, WEIGHTS)
            act.activation(w_vg[:, 0, :, :], raw_vg, ACT.Copy).then_inc(s_wa, 1)
            act.activation(w_e[:, 0, :, :], raw_e, ACT.Copy).then_inc(s_wa, 1)
            act.wait_ge(s_const, CONSTS)

            def exp_unit(b, h, kt, half):
                g = b * HEADS + h
                act.wait_ge(s_st, g * (2 * TT) + (2 * kt + half + 1))
                act.wait_ge(s_pv, g * TT + (kt + 1))
                act.activation(probs[:, kt, half * HALF:(half + 1) * HALF], ps[:, 4 + half, :], ACT.Exp,
                               scale=HD ** -0.5).then_inc(s_p, 1)

            def take_o(b, h):
                g = b * HEADS + h
                act.wait_ge(s_pv, g * TT + 2 * TT)
                act.wait_ge(s_ot, g + 1)
                act.activation(o_sb[:, :], ps[:, 6, 0:T // QUARTERS], ACT.Copy).then_inc(s_o, 1)

            def take_max(b, h):
                g = b * HEADS + h
                act.wait_ge(s_mt, g + 1)
                act.wait_ge(s_md, g * 48 + 16)
                act.activation(m_rows[:, :], ps[0:3 * TT, 7, 0:P], ACT.Copy).then_inc(s_mr, 1)

            def step(b, h, before, turned):
                for kt in range(TT):
                    for half in range(2):
                        exp_unit(b, h, kt, half)
                        if before and kt == 2 and half == 0:
                            take_o(b, h - 1)
                        if turned and kt == 4 and half == 0:
                            take_max(b, h + 1)

            def heads(b):
                step(b, 0, False, True)
                with act.Fori(1, HEADS - 1) as h:
                    step(b, h, True, True)
                step(b, HEADS - 1, True, False)
                take_o(b, HEADS - 1)

            def inv_std(b):
                act.wait_ge(s_mv, b + 1)
                act.activation(rstd[:, :], ln[:, 1, :], ACT.Ln, bias=eps_col[:, :]).then_inc(s_lv, 1)
                act.wait_ge(s_lv, b + 1)
                act.activation(rstd[:, :], rstd[:, :], ACT.Exp, scale=-0.5).then_inc(s_rs, 1)

            def ln_out(b, first, last):
                act.wait_ge(s_rs, b + 1)
                for t in range(first, last):
                    act.activation(att[:, t, :], att[:, t, :], ACT.Identity, bias=ln[:, 0, t:t + 1]).then_inc(s_yc, 1)
                for t in range(first, last):
                    act.wait_ge(s_yc, b * TT + (t + 1))
                    act.activation(att[:, t, :], att[:, t, :], ACT.Copy, scale=rstd[:, t:t + 1]).then_inc(s_y, 1)

            def experts(b, late):
                act.wait_ge(s_gl, b + 1)
                act.activation(gate[:, :, :], gate[:, :, :], ACT.Exp).then_inc(s_ge, 1)
                act.wait_ge(s_cb, b + 1)
                for u in range(1, EU, 2):
                    i = u // 2
                    act.wait_ge(s_ex, b * EU + (u + 1))
                    act.wait_ge(s_pa, b * EU + (2 * i + 2))
                    for e in range(2):
                        mul = act.activation(scaled[:, i % 2, e, :], ps[:, EBANK[u], e * H:(e + 1) * H], ACT.Copy,
                                             scale=comb[:, u // 4, 2 * (u % 4) + e:2 * (u % 4) + e + 1])
                    mul.then_inc(s_ec, 1)
                    if u == 7:
                        act.wait_ge(s_cbt, b + 1)
                        act.activation(combT, pair(0)[0:E, :], ACT.Copy).then_inc(s_cbe, 1)
                    if u == 17 and late is not None:
                        inv_std(late)
                    if u in (19, 21, 23, 25) and late is not None:
                        ln_out(late, u - 19, u - 17)
                    if u == EU - 3:
                        take_max(b, 0)
                act.wait_ge(s_pa, (b + 1) * EU + 4)

            experts(0, None)
            with act.Fori(0, NB - 1) as b:
                heads(b)
                experts(b + 1, b)
            heads(NB - 1)
            inv_std(NB - 1)
            ln_out(NB - 1, 0, TT)

        @block.vector
        def _(dve):
            dve.sem_inc(s_mx, 2)
            dve.sem_inc(s_ot, 1)
            dve.sem_inc(s_nm, 1)
            dve.wait_ge(s_wq, 16 * 3)

            def take_x(b, k):
                dve.wait_ge(s_xt, b * KH + (k + 1))
                dve.tensor_copy(x1T[:, 0, k, :], pair(k)).then_inc(s_xh, 1)
                dve.wait_ge(s_xh, b * KH + (k + 1))
                dve.tensor_tensor(x1T[:, 1, k, :], pair(k), x1T[:, 0, k, :], ALU.subtract).then_inc(s_xte, 1)

            def split_qk(b, mt):
                at = b * (2 * KH * 3) + mt * 3
                bias = b_qk[:, mt:mt + 1]
                part = [qk_parts[:, i, mt % 2, :] for i in range(3)]
                dve.wait_ge(s_qk, b * (2 * KH) + (mt + 1))
                dve.wait_ge(s_qst[mt % 2], b * (16 * KH) + (16 * (mt // 2) + 16))
                dve.tensor_scalar(part[0], pair(mt % 2), bias, None, ALU.add).then_inc(s_sp, 1)
                dve.wait_ge(s_sp, at + 1)
                dve.scalar_tensor_tensor(out=pair(mt % 2), in0=pair(mt % 2), scalar=bias, in1=part[0],
                                         op0=ALU.add, op1=ALU.subtract).then_inc(s_sp, 1)
                dve.wait_ge(s_sp, at + 2)
                dve.tensor_copy(part[1], pair(mt % 2)).then_inc(s_sp, 1)
                dve.wait_ge(s_sp, at + 3)
                dve.tensor_tensor(part[2], pair(mt % 2), part[1], ALU.subtract).then_inc(s_parts, 1)

            def split_max(b, h, stage):
                g = b * HEADS + h
                at = g * 4
                if stage == 0:
                    dve.wait_ge(s_mx, g * TT + (TT + 2))
                    dve.tensor_copy(m_rest[:, 0, :], neg_max[:, :]).then_inc(s_ms, 1)
                    dve.tensor_copy(m_bf[:, 0, :], neg_max[:, :]).then_inc(s_ms, 1)
                if stage == 1:
                    dve.wait_ge(s_ms, at + 2)
                    dve.tensor_tensor(m_rest[:, 1, :], m_rest[:, 0, :], m_bf[:, 0, :], ALU.subtract).then_inc(s_ms, 1)
                    dve.wait_ge(s_mr, g + 1)
                    dve.tensor_copy(m_parts[:, 0, :], m_bf[:, 0, :])
                if stage == 2:
                    dve.wait_ge(s_ms, at + 3)
                    dve.tensor_copy(m_bf[:, 1, :], m_rest[:, 1, :]).then_inc(s_ms, 1)
                if stage == 3:
                    dve.wait_ge(s_ms, at + 4)
                    dve.tensor_copy(m_parts[:, 1, :], m_bf[:, 1, :])
                    dve.tensor_tensor(m_parts[:, 2, :], m_rest[:, 1, :], m_bf[:, 1, :], ALU.subtract).then_inc(s_mp, 1)

            def take_max(b, h, qt, before):
                if before and qt < 4:
                    split_max(b, h - 1, qt)
                    if qt == 0:
                        dve.wait_ge(s_ms, (b * HEADS + h - 1) * 4 + 2)
                dve.wait_ge(s_sc, (b * HEADS + h) * TT + (qt + 1))
                dve.tensor_reduce(neg_max[:, qt:qt + 1], pair(qt % 2), AX.X, ALU.max, negate=True).then_inc(s_mx, 1)

            def normalise(b, h):
                g = b * HEADS + h
                o = ps[:, 7, 0:2 * P].rearrange("p (i j c) -> p i j c", i=2, c=VC)
                to = att[:, :, ds(h * HD, HD)].rearrange("p (j i) c -> p i j c", i=2)
                dve.wait_ge(s_ot, g + 2)
                dve.reciprocal(r_sum[:, :, :, :], o[:, :, :, HD:HD + 1]).then_inc(s_rc, 1)
                dve.wait_ge(s_rc, g + 1)
                dve.tensor_tensor(to, o[:, :, :, 0:HD], r_sum[:, :, :, :].broadcast_to([P, 2, QUARTERS, HD]),
                                  ALU.mult).then_inc(s_nm, 1)

            def step(b, h, before):
                for qt in range(TT):
                    take_max(b, h + PRE, qt, True)
                    if qt == TT - 1 and before:
                        normalise(b, h - 1)

            def heads(b, more):
                dve.wait_ge(s_done, (b + 1) * 16)
                step(b, 0, False)
                with dve.Fori(1, HEADS - PRE) as h:
                    step(b, h, True)
                for stage in range(4):
                    split_max(b, HEADS - 1, stage)
                if more:
                    take_x(b + 1, 0)
                    take_x(b + 1, 1)
                    split_qk(b + 1, 0)
                normalise(b, HEADS - 3)
                if more:
                    for mt in (1, 2, 3):
                        split_qk(b + 1, mt)
                normalise(b, HEADS - 2)
                if more:
                    for t in range(4):
                        take_v(b + 1, t)
                normalise(b, HEADS - 1)
            def add_experts(b, first, last):
                dve.wait_ge(s_nm, (b + 1) * HEADS + 1)
                dve.wait_ge(s_fa, (b + 1) * TT)
                dve.wait_ge(s_eba, (b + 1) * 5)
                dve.tensor_tensor(att[:, first:last, :], att[:, first:last, :], acc[:, first:last, :], ALU.add).then_inc(s_at, 1)

            def ln_sums(b, first, last):
                for t in range(first, last):
                    dve.wait_ge(s_at, b * 4 + (t // 2 + 1))
                    dve.bn_stats(stats[:, t, :], att[:, t, :]).then_inc(s_lns, 1)

            def ln_stats(b):
                dve.wait_ge(s_lns, b * (TT + 5) + TT)
                layer_norm_stats(dve, stats, ln, s_lns, lambda k: b * (TT + 5) + (TT + k)).then_inc(s_mv, 1)

            def take_v(b, t):
                dve.wait_ge(s_v, b * TT + (t + 1))
                v = ps[:, t % 4, :]
                dve.tensor_tensor(v_all[:, t, :], v[:, 0:H], b_vg[:, 0:H], ALU.add)
                dve.tensor_tensor(gate[:, t, :], v[:, H:GV], b_vg[:, H:GV], ALU.add).then_inc(s_ve, 1)

            def experts(b, late):
                for t in range(4, TT):
                    take_v(b, t)
                at = b * 7
                dve.wait_ge(s_ve, (b + 1) * TT)
                dve.tensor_reduce(g_one[:, 0, :], gate[:, :, :], AX.X, ALU.max).then_inc(s_g, 1)
                dve.wait_ge(s_g, at + 1)
                dve.tensor_tensor(gate[:, :, :], gate[:, :, :], g_one[:, 0, :].unsqueeze(2).broadcast_to([P, TT, E]),
                                  ALU.subtract).then_inc(s_gl, 1)
                dve.wait_ge(s_ge, b + 1)
                dve.tensor_reduce(g_one[:, 1, :], gate[:, :, :], AX.X, ALU.add).then_inc(s_g, 1)
                dve.wait_ge(s_g, at + 2)
                dve.reciprocal(g_one[:, 2, :], g_one[:, 1, :]).then_inc(s_g, 1)
                dve.wait_ge(s_g, at + 3)
                dve.tensor_tensor(gate[:, :, :], gate[:, :, :], g_one[:, 2, :].unsqueeze(2).broadcast_to([P, TT, E]),
                                  ALU.mult).then_inc(s_g, 1)
                dve.wait_ge(s_g, at + 4)
                other = gate[:, :, :].unsqueeze(2).broadcast_to([P, TT, E, E])
                own = gate[:, :, :].unsqueeze(3).broadcast_to([P, TT, E, E])
                dve.tensor_tensor(g_cmp[:, 0, :, :, :], other, own, ALU.is_equal).then_inc(s_g, 1)
                dve.tensor_tensor(g_cmp[:, 1, :, :, :], other, own, ALU.is_gt)
                dve.wait_ge(s_g, at + 5)
                dve.tensor_tensor(g_cmp[:, 0, :, :, :], g_cmp[:, 0, :, :, :],
                                  low[:, :, :].unsqueeze(1).broadcast_to([P, TT, E, E]), ALU.mult).then_inc(s_g, 1)
                dve.wait_ge(s_g, at + 6)
                dve.tensor_tensor(g_cmp[:, 0, :, :, :], g_cmp[:, 0, :, :, :], g_cmp[:, 1, :, :, :], ALU.add).then_inc(s_g, 1)
                dve.wait_ge(s_g, at + 7)
                dve.tensor_reduce(g_cmp[:, 1, :, :, 0], g_cmp[:, 0, :, :, :], AX.X, ALU.add).then_inc(s_rk, 1)
                dve.wait_ge(s_rk, b + 1)
                dve.scalar_tensor_tensor(out=comb[:, :, :], in0=g_cmp[:, 1, :, :, 0], scalar=1.5, in1=gate[:, :, :],
                                         op0=ALU.is_lt, op1=ALU.mult).then_inc(s_cb, 1)
                def join(t):
                    dve.wait_ge(s_pa, b * EU + (4 * t + 8))
                    dve.wait_ge(s_ea, b * (EU // 2) + (2 * t + 2))
                    if t == 2:
                        dve.wait_ge(s_eba, (b + 1) * 5)
                    dve.tensor_tensor(acc[:, t, :], acc[:, t, :], x_in[:, t, :], ALU.add).then_inc(s_fa, 1)

                for t in range(TT):
                    if late is not None and t < 4:
                        add_experts(late, 2 * t, 2 * t + 2)
                    for e2 in range(E // 2):
                        u = t * (E // 2) + e2
                        if e2 % 2 == 0:
                            i = b * (EU // 2) + u // 2
                            bank = ps[:, EBANK[u], :]
                            dve.wait_ge(s_ex, b * EU + (u + 1))
                            if e2 == 0:
                                if late is not None:
                                    dve.wait_ge(s_at, late * 4 + (t // 2 + 1))
                                dve.wait_ge(s_cb, b + 1)
                                dve.tensor_scalar(acc[:, t, :], bank[:, 0:H], comb[:, t, 0:1], None, ALU.mult).then_inc(s_es, 1)
                            else:
                                dve.wait_ge(s_ea, i)
                                dve.scalar_tensor_tensor(out=acc[:, t, :], in0=bank[:, 0:H], scalar=comb[:, t, 2 * e2:2 * e2 + 1],
                                                         in1=acc[:, t, :], op0=ALU.mult, op1=ALU.add).then_inc(s_es, 1)
                        if u in EARLY:
                            unit = EARLY.index(u)
                            take_max(b, unit // TT, unit % TT, unit >= TT)
                        if e2 % 2 == 0:
                            dve.wait_ge(s_es, i + 1)
                            dve.scalar_tensor_tensor(out=acc[:, t, :], in0=bank[:, H:2 * H], scalar=comb[:, t, 2 * e2 + 1:2 * e2 + 2],
                                                     in1=acc[:, t, :], op0=ALU.mult, op1=ALU.add).then_inc(s_ea, 1)
                    if t < 4 and late is not None:
                        ln_sums(late, 2 * t, 2 * t + 2)
                    if t == 3 and late is not None:
                        ln_stats(late)
                    if t:
                        join(t - 1)
                    if t == 2:
                        dve.wait_ge(s_eb, b + 1)
                        for to, first, last in ((x_in, 4, 6), (x_in, 6, 8), (x_in, 3, 4), (acc, 2, 3), (acc, 0, 2)):
                            if to is acc and first == 2:
                                dve.wait_ge(s_ea, b * (EU // 2) + 6)
                            if to is acc and first == 0:
                                dve.wait_ge(s_fa, b * TT + 2)
                            to = to[:, first:last, :].rearrange("p t h -> p (t h)")
                            bias = ps[:, first // 2, (first % 2) * H:(first % 2 + last - first) * H]
                            dve.tensor_tensor(to, to, bias, ALU.add).then_inc(s_eba, 1)
                join(TT - 1)

            dve.tensor_copy(w_qk[:, 0, :, :], raw_qk).then_inc(s_wh, 1)
            dve.wait_ge(s_wh, 1)
            dve.tensor_tensor(w_qk[:, 1, :, :], raw_qk, w_qk[:, 0, :, :], ALU.subtract).then_inc(s_ws, 1)
            for k in range(KH):
                take_x(0, k)
            dve.wait_ge(s_wa, 1)
            dve.tensor_tensor(w_vg[:, 1, :, :], raw_vg, w_vg[:, 0, :, :], ALU.subtract).then_inc(s_ws, 1)
            for mt in range(2 * KH):
                split_qk(0, mt)
            dve.wait_ge(s_const, CONSTS)
            dve.wait_ge(s_we, 1)
            for t in range(4):
                take_v(0, t)
            experts(0, None)
            with dve.Fori(0, NB - 1) as b:
                heads(b, True)
                experts(b + 1, b)
            heads(NB - 1, False)
            for i in range(4):
                add_experts(NB - 1, 2 * i, 2 * i + 2)
                ln_sums(NB - 1, 2 * i, 2 * i + 2)
            ln_stats(NB - 1)


def build(nc, d):
    mamba_phase(nc, d)
    attention_phase(nc, d)


def kernel(**inputs):
    import ml_dtypes
    import numpy as np
    import concourse.bacc as bacc
    from concourse.bass_utils import run_bass_kernel_spmd

    a = {k: np.asarray(v) for k, v in inputs.items()}
    x = a["L0_attn_hidden_states"]

    def per_channel(v):
        v = v.reshape((M, P) + v.shape[1:])
        return np.moveaxis(v, 0, 1)

    qkv, bq = a["L0_ffn_W_qkv"], a["L0_ffn_b_qkv"]
    row_sel = np.zeros((3, 2 * NS, 2 * NS, P), np.float32)
    for n in range(2 * NS):
        row_sel[:, n, n, :] = 1.0
    low = np.broadcast_to(np.tril(np.ones((E, E), np.float32), -1), (P, E, E))
    arrays = {
        "x": x, "xT": x.transpose(0, 2, 1),
        "w_in": a["L0_attn_w_in"].T, "w_xp": a["L0_attn_w_xproj"].T, "w_dt": a["L0_attn_w_dt"].T,
        "w_out": a["L0_attn_w_out"].T, "w_conv": per_channel(a["L0_attn_w_conv"][:, 0, :]),
        "b_dt": per_channel(a["L0_attn_b_dt"]), "d": per_channel(a["L0_attn_D"]),
        "a_log": per_channel(a["L0_attn_A_log"]),
        "ident": np.eye(P, dtype=np.float32), "row_sel": row_sel.reshape(3 * 2 * NS, 2 * NS, P).astype(ml_dtypes.bfloat16),
        "w_qk": qkv[:, 0:2 * H], "w_vg": np.concatenate([qkv[:, 2 * H:], a["L0_ffn_W_gate"]], axis=1),
        "b_qk": bq[0:2 * H].reshape(2 * KH, P).T, "b_vg": np.concatenate([bq[2 * H:], a["L0_ffn_b_gate"]])[None, :],
        "w_e": a["L0_ffn_W_experts"].transpose(1, 0, 2).reshape(H, E * H), "b_e": a["L0_ffn_b_experts"],
        "low": low,
    }
    nc = bacc.Bacc("TRN2", target_bir_lowering=False, num_devices=1)
    maps, d = {}, {}
    for name, v in arrays.items():
        v = np.ascontiguousarray(v)
        maps["in_" + name] = v
        d[name] = nc.dram_tensor("in_" + name, v.shape, mybir.dt.from_np(v.dtype), kind="ExternalInput").ap()
    d["out"] = nc.dram_tensor("out", (NB, T, H), F32, kind="ExternalOutput").ap()
    d["x1"] = nc.dram_tensor("x1_scratch", (NB, T, H), F32, kind="Internal").ap()
    d["qk"] = nc.dram_tensor("qk_scratch", (3, 2 * KH * P, T), BF16, kind="Internal").ap()
    build(nc, d)
    r = run_bass_kernel_spmd(nc, [maps], core_ids=[0])
    return r.results[0]["out"]
```
